# Optimizing a Trainium2 kernel written in Bass

```python
import numpy as np
import jax
import jax.numpy as jnp

def _softmax(x, axis=-1):
    return jax.nn.softmax(x, axis=axis)

def _gelu(x):
    return jax.nn.gelu(x, approximate=True)

def _silu(x):
    return jax.nn.silu(x)

def _sigmoid(x):
    return jax.nn.sigmoid(x)

def _layernorm(x, axis=-1, eps=1e-05):
    m = jnp.mean(x, axis=axis, keepdims=True)
    v = jnp.var(x, axis=axis, keepdims=True)
    return (x - m) / jnp.sqrt(v + eps)

def _scatter_add(tgt, idx, src, axis=0):
    return tgt.at[idx].add(src)

def _segment_sum(src, seg, n):
    return jax.ops.segment_sum(src, seg, n)
kernel_name = 'mk_recurrent_d1_jaxref_r8_6d21a3'

def setup_inputs(seed: int=0):
    np.random.seed(seed)
    _w = jnp.asarray

    def _L0_attn_setup():
        import math
        import jax, jax.numpy as jnp
        import numpy as np
        D_MODEL = 128
        N_HEADS = 16
        D_K = D_MODEL // N_HEADS
        THETA = 10000.0

        def _rope(t, cos, sin):
            B, H, S, d = t.shape
            tp = t.reshape(B, H, S, d // 2, 2)
            even, odd = (tp[..., 0], tp[..., 1])
            r_even = even * cos - odd * sin
            r_odd = even * sin + odd * cos
            return jnp.stack([r_even, r_odd], axis=-1).reshape(B, H, S, d)
        key = jax.random.key(seed)
        k1, k2, k3 = jax.random.split(key, 3)
        B, S = (2, 256)
        x = jax.random.normal(k1, (B, S, D_MODEL), dtype=jnp.float32)
        std_qkv = math.sqrt(2.0 / (D_MODEL + 3 * D_MODEL))
        std_out = math.sqrt(2.0 / (D_MODEL + D_MODEL))
        w_qkv = jnp.clip(jax.random.normal(k2, (3 * D_MODEL, D_MODEL), dtype=jnp.float32) * std_qkv, -3 * std_qkv, 3 * std_qkv)
        b_qkv = jnp.zeros((3 * D_MODEL,), dtype=jnp.float32)
        w_out = jnp.clip(jax.random.normal(k3, (D_MODEL, D_MODEL), dtype=jnp.float32) * std_out, -3 * std_out, 3 * std_out)
        b_out = jnp.zeros((D_MODEL,), dtype=jnp.float32)
        return {'x': x, 'w_qkv': w_qkv, 'b_qkv': b_qkv, 'w_out': w_out, 'b_out': b_out}
    _L0_attn_in = _L0_attn_setup()

    def _L0_ffn_setup():
        import jax, jax.numpy as jnp
        import numpy as np
        EPS = 1e-05

        def _quantize(W):
            gamma = jnp.mean(jnp.abs(W))
            return jnp.clip(jnp.round(W / (gamma + EPS)), -1.0, 1.0)
        key = jax.random.key(seed)
        k_x, k_w1, k_b1, k_w2, k_b2 = jax.random.split(key, 5)
        n_embd = 128
        d_ff = 4 * n_embd
        B, S = (4, 512)
        bound1 = 1.0 / np.sqrt(n_embd)
        bound2 = 1.0 / np.sqrt(d_ff)
        x = jax.random.normal(k_x, (B, S, n_embd), dtype=jnp.float32)
        W1 = jax.random.uniform(k_w1, (d_ff, n_embd), jnp.float32, -bound1, bound1)
        b1 = jax.random.uniform(k_b1, (d_ff,), jnp.float32, -bound1, bound1)
        W2 = jax.random.uniform(k_w2, (n_embd, d_ff), jnp.float32, -bound2, bound2)
        b2 = jax.random.uniform(k_b2, (n_embd,), jnp.float32, -bound2, bound2)
        return {'x': x, 'W1': W1, 'b1': b1, 'W2': W2, 'b2': b2}
    _L0_ffn_in = _L0_ffn_setup()
    _d = {'L0_attn_x': _L0_attn_in['x'], 'L0_attn_w_qkv': _L0_attn_in['w_qkv'], 'L0_attn_b_qkv': _L0_attn_in['b_qkv'], 'L0_attn_w_out': _L0_attn_in['w_out'], 'L0_attn_b_out': _L0_attn_in['b_out'], 'L0_ffn_W1': _L0_ffn_in['W1'], 'L0_ffn_b1': _L0_ffn_in['b1'], 'L0_ffn_W2': _L0_ffn_in['W2'], 'L0_ffn_b2': _L0_ffn_in['b2']}
    _x0 = _d['L0_attn_x']
    _d['L0_attn_x'] = jax.random.normal(jax.random.fold_in(jax.random.key(seed), 1), (16, 256, 128), dtype=_x0.dtype)
    del _x0
    return _d

def reference(L0_attn_x, L0_attn_w_qkv, L0_attn_b_qkv, L0_attn_w_out, L0_attn_b_out, L0_ffn_W1, L0_ffn_b1, L0_ffn_W2, L0_ffn_b2):

    def _L0_attn_ref(x, w_qkv, b_qkv, w_out, b_out):
        import math
        import jax, jax.numpy as jnp
        import numpy as np
        D_MODEL = 128
        N_HEADS = 16
        D_K = D_MODEL // N_HEADS
        THETA = 10000.0

        def _rope(t, cos, sin):
            B, H, S, d = t.shape
            tp = t.reshape(B, H, S, d // 2, 2)
            even, odd = (tp[..., 0], tp[..., 1])
            r_even = even * cos - odd * sin
            r_odd = even * sin + odd * cos
            return jnp.stack([r_even, r_odd], axis=-1).reshape(B, H, S, d)
        B, S, _ = x.shape
        qkv = jnp.einsum('bsi,oi->bso', x, w_qkv) + b_qkv
        qkv = qkv.reshape(B, S, 3, N_HEADS, D_K).transpose(2, 0, 3, 1, 4)
        q, k, v = (qkv[0], qkv[1], qkv[2])
        inv_freq = THETA ** (-jnp.arange(0, D_K, 2, dtype=jnp.float32) / D_K)
        ang = jnp.arange(S, dtype=jnp.float32)[:, None] * inv_freq[None, :]
        cos, sin = (jnp.cos(ang), jnp.sin(ang))
        q = _rope(q, cos, sin)
        k = _rope(k, cos, sin)
        scale = 1.0 / math.sqrt(D_K)
        scores = jnp.einsum('bhqd,bhkd->bhqk', q.astype(jnp.float32), k.astype(jnp.float32)) * scale
        causal = jnp.tril(jnp.ones((S, S), dtype=bool))
        scores = jnp.where(causal, scores, jnp.finfo(jnp.float32).min)
        ex = jnp.exp(scores - jnp.max(scores, axis=-1, keepdims=True))
        attn = ex / (jnp.sum(ex, axis=-1, keepdims=True) + 1e-08)
        attn = attn.astype(v.dtype)
        o = jnp.einsum('bhqk,bhkd->bhqd', attn, v)
        o = o.transpose(0, 2, 1, 3).reshape(B, S, D_MODEL)
        out = jnp.einsum('bsi,oi->bso', o, w_out) + b_out
        return out

    def _L0_ffn_ref(x, W1, b1, W2, b2):
        import jax, jax.numpy as jnp
        import numpy as np
        EPS = 1e-05

        def _quantize(W):
            gamma = jnp.mean(jnp.abs(W))
            return jnp.clip(jnp.round(W / (gamma + EPS)), -1.0, 1.0)
        Wq1 = _quantize(W1)
        Wq2 = _quantize(W2)
        h = jax.nn.relu(jnp.einsum('bsd,fd->bsf', x, Wq1) + b1)
        out = jnp.einsum('bsf,df->bsd', h, Wq2) + b2
        return out
    x = L0_attn_x
    xn = _layernorm(x, axis=-1)
    s = _L0_attn_ref(xn, L0_attn_w_qkv, L0_attn_b_qkv, L0_attn_w_out, L0_attn_b_out)
    g = _silu(_L0_ffn_ref(xn, L0_ffn_W1, L0_ffn_b1, L0_ffn_W2, L0_ffn_b2))
    x = x + s * g
    return x

_drawn_inputs = setup_inputs


def setup_inputs(seed=0):
    import zlib

    import numpy as np

    out = dict(_drawn_inputs(seed))
    spreads = {'L0_attn_b_qkv': (0.0, 0.1), 'L0_attn_b_out': (0.0, 0.1)}
    factors = {'L0_ffn_b1': 8.0, 'L0_ffn_b2': 200.0}
    for name, (base, spread) in spreads.items():
        noise = np.random.default_rng([zlib.crc32(name.encode()), seed]).standard_normal(out[name].shape)
        drawn = base * np.exp(spread * noise) if base else spread * noise
        out[name] = jnp.asarray(drawn.astype(out[name].dtype))
    for name, factor in factors.items():
        out[name] = (out[name] * factor).astype(out[name].dtype)
    return out
```

```python
from contextlib import ExitStack

import concourse.bass as bass
from concourse import mybir

F32 = mybir.dt.float32
BF16 = mybir.dt.bfloat16
F16 = mybir.dt.float16
ALU = mybir.AluOpType
ACT = mybir.ActivationFunctionType
AX_X = mybir.AxisListType.X

P = 128
DK = 8
QUAD = 32
LN_EPS = 1e-5
Q_EPS = 1e-5
SUM_EPS = 1e-8
Z_MIN = -87.0
MASKED = -1e30
PRODUCTS = [(0, 0), (0, 1), (0, 2), (1, 0), (1, 1), (2, 0)]
PARTS = 3
ROWS = DK * len(PRODUCTS)
SHIFT_ROWS = ROWS + PARTS
AHEAD = 4

STEPS = 12
C_START = 6


def attention_ffn_gate(nc, x, w_qkv_t, b_qkv_all, w_out_t, b_out_col, w1_t, w1_rows, b1_cols,
                       w2_t, w2_rows, b2_col, ident_in, mask_in, rope_in, out):
    B, S, D = x.shape
    T = S // P
    H = D // DK
    F = w1_t.shape[1]
    FB = F // P
    G = H // 4
    SCALE = float(DK) ** -0.5
    NT = B * T
    HEADW = DK + 1
    assert T == 2 and D == P and G == 4 and FB == 4 and 3 * G == STEPS

    UNITS = [(g, kb, qb) for g in range(G) for kb, qb in ((0, 0), (0, 1), (1, 1))]
    NU = len(UNITS)

    with ExitStack() as ctx:
        def sb(name, shape, dt=F32):
            return ctx.enter_context(nc.sbuf_tensor(name, shape, dt))

        def sem(name):
            return ctx.enter_context(nc.semaphore(name))

        ident = sb("ident", [P, P])
        ident_bf = sb("ident_bf", [P, P], BF16)
        mask = sb("mask", [P, P])
        mask_bf = sb("mask_bf", [P, P], BF16)
        rope = sb("rope", [P, T, 16])
        ones = sb("ones", [P, P])
        wqkv = sb("wqkv", [P, 3 * D])
        bqkv = sb("bqkv", [P, 3 * D])
        wout = sb("wout", [P, D])
        bout = sb("bout", [P, 1])
        w1 = sb("w1", [P, F])
        w1n = sb("w1n", [P, FB, D])
        w2 = sb("w2", [P, FB, D])
        w2n = sb("w2n", [P, F])
        b1 = sb("b1", [P, FB])
        b2 = sb("b2", [P, 1])
        wabs = sb("wabs", [P, 2])
        gam = sb("gam", [P, 2])
        thr = sb("thr", [P, 2, 2])
        lowq = sb("lowq", [P, 2, F])
        w1q = sb("w1q", [P, F], F16)
        w2q = sb("w2q", [P, FB, D])
        xs = sb("xs", [P, NT, D])
        stats = sb("stats", [P, NT, 6])
        mv = sb("mv", [P, NT, 2])
        std = sb("std", [P, NT])
        rstd = sb("rstd", [P, NT])
        xn = sb("xn", [P, T, D])
        xnT = sb("xnT", [P, 2, S])
        xnT_hi = sb("xnT_hi", [P, AHEAD, S], F16)
        xnT_lo = sb("xnT_lo", [P, AHEAD, S], F16)
        qk = sb("qk", [P, T, 2 * D])
        vaug = sb("vaug", [P, AHEAD, T, H, HEADW])
        rot_a = sb("rot_a", [P, T, 2 * D])
        rot_b = sb("rot_b", [P, T, 2 * D])
        rot = sb("rot", [P, T, 2 * D])
        rem = sb("rem", [P, T, 2 * D])
        parts = sb("parts", [P, PARTS, T, 2, D], BF16)
        partsT = sb("partsT", [P, 2, PARTS, S], BF16)
        qstack = sb("qstack", [P, AHEAD, H, S], BF16)
        kstack = sb("kstack", [P, AHEAD, H, S], BF16)
        mx = sb("mx", [P, 3, H])
        mrem = sb("mrem", [P, T, H])
        mparts = sb("mparts", [P, T, P // H, H], BF16)
        mT = sb("mT", [PARTS * H, S], BF16)
        probs = sb("probs", [P, NU, 4, P])
        oT = sb("oT", [P, G, S])
        lsum = sb("lsum", [P, T, H])
        linv = sb("linv", [P, T, H])
        onorm = sb("onorm", [P, T, D])
        onT = sb("onT", [P, S])
        hT = sb("hT", [P, FB, S])
        zc = sb("zc", [P, S])
        e_z = sb("e_z", [P, S])
        den = sb("den", [P, S])
        sig = sb("sig", [P, S])
        gT = sb("gT", [P, AHEAD, S])
        sg = sb("sg", [P, S])
        res = sb("res", [P, 2, T, D])

        s1 = ctx.enter_context(nc.psum_tensor("s1", [P, 2, 512], F32))
        s2 = ctx.enter_context(nc.psum_tensor("s2", [P, 2, 512], F32))
        pv = ctx.enter_context(nc.psum_tensor("pv", [P, 2, 512], F32))
        misc = ctx.enter_context(nc.psum_tensor("misc", [P, 2, 512], F32))

        x_loaded = [sem(f"x_loaded{i}") for i in range(2)]
        consts_loaded = sem("consts_loaded")
        weights_loaded = sem("weights_loaded")
        spread_out = [sem(f"spread_out{i}") for i in range(2)]
        stacks_loaded = [sem(f"stacks_loaded{i}") for i in range(2)]
        shifts_loaded = sem("shifts_loaded")
        stored = [sem(f"stored{i}") for i in range(2)]
        stack_ones = sem("stack_ones")
        consts_ready = sem("consts_ready")
        abs_ready = sem("abs_ready")
        gamma_sum = sem("gamma_sum")
        quant_step = sem("quant_step")
        weights_ready = sem("weights_ready")
        pv_zeroed = sem("pv_zeroed")
        stat_step = sem("stat_step")
        std_ready = sem("std_ready")
        rstd_ready = sem("rstd_ready")
        xn_ready = sem("xn_ready")
        xnT_ps = sem("xnT_ps")
        xnT_ready = sem("xnT_ready")
        xnT_hi_ready = sem("xnT_hi_ready")
        xnT_lo_ready = sem("xnT_lo_ready")
        qkv_ps = sem("qkv_ps")
        qk_ready = sem("qk_ready")
        v_ready = sem("v_ready")
        v_ones = sem("v_ones")
        mmax_ready = sem("mmax_ready")
        rope_terms = sem("rope_terms")
        rotated = sem("rotated")
        part_hi = sem("part_hi")
        part_rem = sem("part_rem")
        part_mid = sem("part_mid")
        part_lo = sem("part_lo")
        partsT_ps = sem("partsT_ps")
        partsT_ready = sem("partsT_ready")
        s1_ps = sem("s1_ps")
        max_ready = sem("max_ready")
        shift_step = sem("shift_step")
        mT_ps = sem("mT_ps")
        mT_ready = sem("mT_ready")
        s2_ps = sem("s2_ps")
        exp_ready = sem("exp_ready")
        exp_seen = sem("exp_seen")
        causal_ready = sem("causal_ready")
        pv_ps = sem("pv_ps")
        oT_ready = sem("oT_ready")
        o_ps = sem("o_ps")
        sum_ready = sem("sum_ready")
        onorm_ready = sem("onorm_ready")
        onT_ps = sem("onT_ps")
        onT_ready = sem("onT_ready")
        h_ps = sem("h_ps")
        h_ready = sem("h_ready")
        z_ps = sem("z_ps")
        zc_ready = sem("zc_ready")
        e_ready = sem("e_ready")
        silu_step = sem("silu_step")
        g_ready = sem("g_ready")
        s_ps = sem("s_ps")
        sg_ready = sem("sg_ready")
        sgT_ps = sem("sgT_ps")
        res_ready = sem("res_ready")

        JOBS = [
            (0, 0, "xnT", [(xnT_ready, 1, 1), (xnT_hi_ready, 1, 1)]),
            (0, 4, "proj", [(sg_ready, 1, 1)]),
            (1, 2, "shift", [(mT_ready, 1, 1)]),
            (1, 0, "qkv0", [(qk_ready, 2, 1), (v_ready, 2, 1)]),
            (1, 0, "qkv1", [(qk_ready, 2, 2), (v_ready, 2, 2)]),
            (2, 4, "back", [(res_ready, 1, 1)]),
            (3, 2, "h0", [(h_ready, FB, 2)]),
            (4, 2, "h1", [(h_ready, FB, 4)]),
            (6, 2, "z", [(g_ready, 1, 1)]),
            (8, 0, "partsq", [(partsT_ready, 2, 1)]),
            (8, 0, "partsk", [(partsT_ready, 2, 2)]),
            (10, 3, "o1", [(onorm_ready, 1, 1)]),
            (10, 3, "o0", [(onorm_ready, 1, 1)]),
            (11, 3, "onT", [(onT_ready, 1, 1)]),
        ]
        BANK = {name: n % 2 for n, (_, _, name, _) in enumerate(JOBS)}
        assert (BANK["o0"], BANK["o1"]) == (0, 1)
        NJ = len(JOBS)

        def events(table, t, known):
            for row in table:
                if 0 <= known - row[1] < B:
                    yield (t - row[1], known - row[1], *row)

        def iterations(eng, body):
            for t in range(AHEAD):
                body(t, t)
            with eng.Fori(AHEAD, B - AHEAD + 1, AHEAD) as t0:
                for j in range(AHEAD):
                    body(t0 + j, AHEAD + j)
            for t in range(B, B + AHEAD):
                body(t, t)

        def second_pass(t, known, step):
            lag, u = (2, step - C_START) if step >= C_START else (3, step - C_START + STEPS)
            return (t - lag, known - lag, u) if 0 <= known - lag < B else None

        scratch = nc.dram_tensor("scratch", [2, 2, ROWS, H, S], BF16, kind="Internal").ap()

        block = ctx.enter_context(nc.Block())

        @block.sync
        def _(sp):
            half = NT // 2
            xt = x.rearrange("b (i p) d -> p (b i) d", p=P)
            sp.dma_start(xs[:, 0:half, :], xt[:, 0:half, :]).then_inc(x_loaded[0], 16)
            for dst, src in ((ident, ident_in), (mask, mask_in), (rope, rope_in)):
                sp.dma_start(dst[:], src).then_inc(consts_loaded, 16)
            for dst, src in ((wqkv, w_qkv_t), (bqkv, b_qkv_all), (wout, w_out_t), (bout, b_out_col),
                             (w1, w1_t), (w1n, w1_rows), (w2, w2_t), (w2n, w2_rows), (b1, b1_cols),
                             (b2, b2_col)):
                sp.dma_start(dst[:], src).then_inc(weights_loaded, 16)
            sp.dma_start(xs[:, half:NT, :], xt[:, half:NT, :]).then_inc(x_loaded[1], 16)
            sp.wait_ge(stack_ones, 1)

            def spread(b, kb, side):
                sp.wait_ge(partsT_ready, 2 * b + 1 + side)
                for n, pair in enumerate(PRODUCTS):
                    dst = scratch[kb % 2, side, DK * n:DK * (n + 1), :, :].rearrange("d h s -> h d s")
                    sp.dma_start(dst, partsT[:, side, pair[side], :]).then_inc(spread_out[side], 16)

            def stack(b, kb, side):
                sp.wait_ge(spread_out[side], 16 * len(PRODUCTS) * (b + 1))
                sp.dma_start((kstack if side else qstack)[0:ROWS, kb % AHEAD, :, :],
                             scratch[kb % 2, side, :, :, :]).then_inc(stacks_loaded[kb % 2], 16)

            def shift(b, kb):
                sp.wait_ge(mT_ready, b + 1)
                for c in range(PARTS):
                    sp.dma_start(qstack[ROWS + c:ROWS + c + 1, kb % AHEAD, :, :],
                                 mT[H * c:H * (c + 1), :]).then_inc(shifts_loaded, 16)

            def store(b, kb):
                sp.wait_ge(res_ready, b + 1)
                sp.dma_start(out[bass.ds(b, 1), :, :].rearrange("o (i p) d -> p (o i) d", p=P),
                             res[:, kb % 2, :, :]).then_inc(stored[kb % 2], 16)

            def iteration(t, known):
                for b, kb, *_ in events([(0, 2)], t, known):
                    shift(b, kb)
                for b, kb, *_ in events([(3, 4)], t, known):
                    store(b, kb)
                for b, kb, *_ in events([(8, 0)], t, known):
                    spread(b, kb, 0)
                    spread(b, kb, 1)
                    stack(b, kb, 0)
                    stack(b, kb, 1)

            iterations(sp, iteration)
            for s in stored:
                sp.wait_ge(s, 16 * B // 2)

        @block.tensor
        def _(pe):
            pe.wait_ge(abs_ready, 3)
            nc.tensor.matmul(misc[:, 0, 0:2], ones[:, :], wabs[:, :], start=True, stop=True).then_inc(gamma_sum, 1)
            pe.wait_ge(weights_ready, 2)
            pe.wait_ge(consts_ready, 2)
            pe.wait_ge(pv_zeroed, 1)
            pe.wait_ge(weights_loaded, 160)

            def job_bank(n, t, known):
                for back in range(2, 4 * NJ, 2):
                    m, it = (n - back) % NJ, (n - back) // NJ
                    lag = JOBS[m][1]
                    if 0 <= known + it - lag < B:
                        for s, per, at in JOBS[m][3]:
                            pe.wait_ge(s, per * (t + it - lag) + at)
                        return

            def job(n, t, known, name, b, kb):
                bank = misc[:, BANK[name], :]
                job_bank(n, t, known)
                buf = kb % AHEAD
                if name == "xnT":
                    pe.wait_ge(xn_ready, 2 * b + 2)
                    for i in range(T):
                        mm = nc.tensor.transpose(bank[:, P * i:P * (i + 1)], xn[:, i, :], ident[:, :])
                    mm.then_inc(xnT_ps, 1)
                elif name in ("qkv0", "qkv1"):
                    i = int(name[-1])
                    pe.wait_ge(xnT_ready, b + 1)
                    nc.tensor.matmul(bank[:, 0:3 * D], xnT[:, kb % 2, P * i:P * (i + 1)], wqkv[:, :],
                                     start=True, stop=True).then_inc(qkv_ps, 1)
                elif name in ("partsq", "partsk"):
                    side = name == "partsk"
                    pe.wait_ge(part_lo, b + 1)
                    dst = bank.bitcast(BF16).rearrange("p (c s) -> p c s", s=S)
                    for c in range(PARTS):
                        for i in range(T):
                            mm = nc.tensor.transpose(dst[:, c, P * i:P * (i + 1)], parts[:, c, i, int(side), :],
                                                     ident_bf[:, :])
                    mm.then_inc(partsT_ps, 1)
                elif name == "shift":
                    pe.wait_ge(shift_step, 4 * b + 4)
                    dst = bank.bitcast(BF16)
                    for i in range(T):
                        mm = nc.tensor.transpose(dst[:, P * i:P * (i + 1)],
                                                 mparts[:, i, :, :].rearrange("p c h -> p (c h)"), ident_bf[:, :])
                    mm.then_inc(mT_ps, 1)
                elif name in ("h0", "h1"):
                    pe.wait_ge(xnT_lo_ready, b + 1)
                    pe.wait_ge(xnT_hi_ready, b + 1)
                    for f in range(2):
                        w = w1q[:, P * (2 * int(name[-1]) + f):P * (2 * int(name[-1]) + f + 1)]
                        for k, part in enumerate((xnT_hi, xnT_lo)):
                            mm = nc.tensor.matmul(bank[:, S * f:S * (f + 1)], w, part[:, buf, :],
                                                  start=k == 0, stop=k == 1)
                    mm.then_inc(h_ps, 1)
                elif name == "z":
                    pe.wait_ge(h_ready, FB * b + FB)
                    for f in range(FB):
                        mm = nc.tensor.matmul(bank[:, 0:S], w2q[:, f, :], hT[:, f, :], start=f == 0, stop=f == FB - 1)
                    mm.then_inc(z_ps, 1)
                elif name in ("o0", "o1"):
                    i = int(name[-1])
                    pe.wait_ge(oT_ready, G * b + G)
                    for g in range(G):
                        mm = nc.tensor.transpose(bank[:, P * g:P * (g + 1)], oT[:, g, P * i:P * (i + 1)], ident[:, :])
                    mm.then_inc(o_ps, 1)
                elif name == "onT":
                    pe.wait_ge(onorm_ready, b + 1)
                    for i in range(T):
                        mm = nc.tensor.transpose(bank[:, P * i:P * (i + 1)], onorm[:, i, :], ident[:, :])
                    mm.then_inc(onT_ps, 1)
                elif name == "proj":
                    pe.wait_ge(onT_ready, b + 1)
                    nc.tensor.matmul(bank[:, 0:S], wout[:, :], onT[:, :], start=True, stop=True).then_inc(s_ps, 1)
                elif name == "back":
                    pe.wait_ge(sg_ready, b + 1)
                    for i in range(T):
                        mm = nc.tensor.transpose(bank[:, P * i:P * (i + 1)], sg[:, P * i:P * (i + 1)], ident[:, :])
                    mm.then_inc(sgT_ps, 1)

            def pass1(b, kb, u, known):
                g, key, query = UNITS[u]
                if u == 0:
                    pe.wait_ge(stacks_loaded[kb % 2], 16 * (b - kb % 2) + 32)
                if kb > 0 or u >= 2:
                    pe.wait_ge(max_ready, NU * b + u - 1)
                bank = s1[:, u % 2, :]
                diagonal = key == query
                if diagonal:
                    nc.tensor.matmul(bank.rearrange("p (h k) -> p h k", h=4), ident_bf[:, :],
                                     mask_bf[:, :].unsqueeze(1).broadcast_to([P, 4, P]), start=True, stop=False)
                for j in range(4):
                    h = 4 * g + j
                    mm = nc.tensor.matmul(bank[:, P * j:P * (j + 1)],
                                          qstack[0:ROWS, kb % AHEAD, h, P * query:P * (query + 1)],
                                          kstack[0:ROWS, kb % AHEAD, h, P * key:P * (key + 1)],
                                          start=not diagonal, stop=not diagonal or j == 3)
                mm.then_inc(s1_ps, 1)

            def pass2(b, kb, u):
                g, key, query = UNITS[u]
                if u == 0:
                    pe.wait_ge(shifts_loaded, 16 * PARTS * (b + 1))
                if kb > 0 or u >= 2:
                    pe.wait_ge(exp_ready, NU * b + u - 1)
                for j in range(4):
                    h = 4 * g + j
                    mm = nc.tensor.matmul(s2[:, u % 2, P * j:P * (j + 1)],
                                          kstack[0:SHIFT_ROWS, kb % AHEAD, h, P * key:P * (key + 1)],
                                          qstack[0:SHIFT_ROWS, kb % AHEAD, h, P * query:P * (query + 1)],
                                          start=True, stop=True)
                mm.then_inc(s2_ps, 1)

            def weigh(b, kb, g):
                pe.wait_ge(causal_ready, 2 * G * b + 2 * g + 2)
                pe.wait_ge(exp_ready, NU * b + 3 * g + 3)
                pe.wait_ge(v_ready, 2 * b + 2)
                if kb > 0 or g >= 2:
                    pe.wait_ge(oT_ready, G * b + g - 1)
                for j in range(4):
                    nc.tensor.matmul(pv[QUAD * j:QUAD * j + HEADW, g % 2, 0:S], vaug[:, kb % AHEAD, 0, 4 * g + j, :],
                                     probs[:, 3 * g:3 * g + 2, j, :], start=True, stop=False)
                for j in range(4):
                    mm = nc.tensor.matmul(pv[QUAD * j:QUAD * j + HEADW, g % 2, P:S], vaug[:, kb % AHEAD, 1, 4 * g + j, :],
                                          probs[:, 3 * g + 2, j, :], start=False, stop=True)
                mm.then_inc(pv_ps, 1)

            WEIGH = [(2, 3, 1), (5, 3, 2), (8, 3, 3), (11, 2, 0)]

            def iteration(t, known):
                for step in range(STEPS):
                    if 0 <= known - 1 < B:
                        pass1(t - 1, known - 1, step, known)
                    if (c := second_pass(t, known, step)) is not None:
                        pass2(*c)
                    for n, row in enumerate(JOBS):
                        if row[0] == step:
                            for b, kb, *_ in events([row], t, known):
                                job(n, t, known, row[2], b, kb)
                    for b, kb, at, _, g in events(WEIGH, t, known):
                        if at == step:
                            weigh(b, kb, g)

            iterations(pe, iteration)

        @block.vector
        def _(dve):
            dve.memset(ones[:, :], 1.0).then_inc(abs_ready, 1)
            dve.memset(kstack[32:64, :, :, :], 1.0).then_inc(stack_ones, 1)
            dve.memset(vaug[:, :, :, :, DK:HEADW], 1.0).then_inc(v_ones, 1)
            dve.memset(pv[:, :, :], 0.0).then_inc(pv_zeroed, 1)
            dve.memset(mparts[:, :, :, :], 0.0).then_inc(mmax_ready, 1)
            dve.wait_ge(consts_loaded, 48)
            dve.tensor_copy(ident_bf[:, :], ident[:, :]).then_inc(consts_ready, 1)
            dve.tensor_copy(mask_bf[:, :], mask[:, :]).then_inc(consts_ready, 1)
            dve.wait_ge(weights_loaded, 160)
            nc.vector.tensor_reduce(wabs[:, 0:1], w1n[:, :, :], axis=mybir.AxisListType.XY, op=ALU.add,
                                    apply_absolute_value=True).then_inc(abs_ready, 1)
            nc.vector.tensor_reduce(wabs[:, 1:2], w2n[:, :], axis=AX_X, op=ALU.add,
                                    apply_absolute_value=True).then_inc(abs_ready, 1)
            dve.wait_ge(gamma_sum, 1)
            dve.tensor_scalar(gam[:, :], misc[:, 0, 0:2], 1.0 / (F * D), Q_EPS, ALU.mult, ALU.add).then_inc(quant_step, 1)
            dve.wait_ge(quant_step, 1)
            dve.tensor_scalar(thr[:, 0, :], gam[:, :], 0.5, None, ALU.mult).then_inc(quant_step, 1)
            dve.tensor_scalar(thr[:, 1, :], gam[:, :], -0.5, None, ALU.mult).then_inc(quant_step, 1)
            dve.wait_ge(quant_step, 3)
            w2flat = w2[:, :, :].rearrange("p f d -> p (f d)")
            w2qflat = w2q[:, :, :].rearrange("p f d -> p (f d)")
            for n, (w, q) in enumerate(((w1[:, :], w1q[:, :]), (w2flat, w2qflat))):
                dve.tensor_scalar(lowq[:, n, :], w, thr[:, 1, n:n + 1], None, ALU.is_lt).then_inc(quant_step, 1)
                dve.wait_ge(quant_step, 4 + n)
                nc.vector.scalar_tensor_tensor(q, w, thr[:, 0, n:n + 1], lowq[:, n, :], ALU.is_gt,
                                               ALU.subtract).then_inc(weights_ready, 1)
            for tile in range(NT):
                if tile % (NT // 2) == 0:
                    dve.wait_ge(x_loaded[tile // (NT // 2)], 16)
                nc.vector.bn_stats(stats[:, tile, :], xs[:, tile, :]).then_inc(stat_step, 1)
            dve.wait_ge(stat_step, NT)
            for tile in range(NT):
                nc.vector.bn_aggr(mv[:, tile, :], stats[:, tile, :]).then_inc(stat_step, 1)
            dve.wait_ge(stat_step, 2 * NT)
            dve.tensor_scalar(mv[:, :, 1], mv[:, :, 1], LN_EPS, None, ALU.add).then_inc(stat_step, 1)
            dve.wait_ge(std_ready, 1)
            nc.vector.reciprocal(rstd[:, :], std[:, :]).then_inc(rstd_ready, 1)
            dve.wait_ge(rstd_ready, 1)
            dve.wait_ge(v_ones, 1)

            def maxima(b, kb, u):
                g, key, query = UNITS[u]
                dve.wait_ge(s1_ps, NU * b + u + 1)
                if u == 0 and kb > 0:
                    dve.wait_ge(shift_step, 4 * b)
                slot = {(0, 0): 0, (1, 1): 1, (0, 1): 2}[(key, query)]
                nc.vector.tensor_reduce(mx[:, slot, 4 * g:4 * g + 4], s1[:, u % 2, :].rearrange("p (h k) -> p h k", h=4),
                                        axis=AX_X, op=ALU.max).then_inc(max_ready, 1)

            def normalise(b, kb):
                if kb > 0:
                    dve.wait_ge(xnT_ps, b)
                for i in range(T):
                    tile = T * b + i
                    ti = bass.ds(tile, 1)
                    dve.tensor_scalar(xn[:, i:i + 1, :], xs[:, ti, :], mv_of(tile), rstd_of(tile),
                                      ALU.subtract, ALU.mult).then_inc(xn_ready, 1)

            def mv_of(tile):
                return mv[:, bass.ds(tile, 1), 0]

            def rstd_of(tile):
                return rstd[:, bass.ds(tile, 1)]

            def qkv(b, kb, i):
                dve.wait_ge(qkv_ps, 2 * b + i + 1)
                if kb > 0:
                    dve.wait_ge(part_lo, b)
                bank = misc[:, BANK[f"qkv{i}"], :]
                dve.tensor_tensor(qk[:, i, :], bank[:, 0:2 * D], bqkv[:, 0:2 * D], ALU.add).then_inc(qk_ready, 1)
                if kb >= AHEAD:
                    dve.wait_ge(pv_ps, G * (b - AHEAD + 1))
                dve.tensor_tensor(vaug[:, kb % AHEAD, i, :, 0:DK],
                                  bank[:, 2 * D:3 * D].rearrange("p (h d) -> p h d", d=DK),
                                  bqkv[:, 2 * D:3 * D].rearrange("p (h d) -> p h d", d=DK), ALU.add).then_inc(v_ready, 1)

            def partsT_copy(b, kb, side):
                dve.wait_ge(partsT_ps, 2 * b + side + 1)
                if kb > 0:
                    dve.wait_ge(spread_out[side], 16 * len(PRODUCTS) * b)
                name = ("partsq", "partsk")[side]
                dve.tensor_copy(partsT[:, side, :, :],
                                misc[:, BANK[name], :].bitcast(BF16)[:, 0:PARTS * S].rearrange("p (c s) -> p c s", c=PARTS)
                                ).then_inc(partsT_ready, 1)

            def shift(b, kb):
                dve.wait_ge(max_ready, NU * b + NU)
                if kb > 0:
                    dve.wait_ge(mT_ps, b)
                dve.tensor_tensor(mx[:, 1, :], mx[:, 1, :], mx[:, 2, :], ALU.max).then_inc(mmax_ready, 1)
                dve.wait_ge(mmax_ready, b + 2)
                m = mx[:, 0:2, :]
                dve.tensor_scalar(mparts[:, :, 0, :], m, -1.0, None, ALU.mult).then_inc(shift_step, 1)
                dve.wait_ge(shift_step, 4 * b + 1)
                nc.vector.scalar_tensor_tensor(mrem[:, :, :], m, -1.0, mparts[:, :, 0, :], ALU.mult,
                                               ALU.subtract).then_inc(shift_step, 1)
                dve.wait_ge(shift_step, 4 * b + 2)
                dve.tensor_copy(mparts[:, :, 1, :], mrem[:, :, :]).then_inc(shift_step, 1)
                dve.wait_ge(shift_step, 4 * b + 3)
                dve.tensor_tensor(mparts[:, :, 2, :], mrem[:, :, :], mparts[:, :, 1, :], ALU.subtract).then_inc(shift_step, 1)

            def mT_copy(b, kb):
                dve.wait_ge(mT_ps, b + 1)
                if kb > 0:
                    dve.wait_ge(shifts_loaded, 16 * PARTS * b)
                dve.tensor_copy(mT[:, :], misc[0:PARTS * H, BANK["shift"], :].bitcast(BF16)[:, 0:S]).then_inc(mT_ready, 1)

            def onorm_make(b, kb):
                dve.wait_ge(o_ps, 2 * b + 2)
                heads = misc[:, :, :].rearrange("p i (h w) -> p i h w", w=QUAD)
                if kb > 0:
                    dve.wait_ge(onT_ps, b)
                dve.tensor_scalar(lsum[:, :, :], heads[:, :, :, DK], SUM_EPS, None, ALU.add).then_inc(sum_ready, 1)
                dve.wait_ge(sum_ready, 2 * b + 1)
                nc.vector.reciprocal(linv[:, :, :], lsum[:, :, :]).then_inc(sum_ready, 1)
                dve.wait_ge(sum_ready, 2 * b + 2)
                dve.tensor_tensor(onorm[:, :, :].rearrange("p i (h d) -> p (i h) d", d=DK),
                                  heads[:, :, :, 0:DK].rearrange("p i h d -> p (i h) d"),
                                  linv[:, :, :].rearrange("p i h -> p (i h)").unsqueeze(2).broadcast_to([P, T * H, DK]),
                                  ALU.mult).then_inc(onorm_ready, 1)

            def clamp(b, kb):
                dve.wait_ge(z_ps, b + 1)
                if kb > 0:
                    dve.wait_ge(e_ready, b)
                dve.tensor_scalar(zc[:, :], misc[:, BANK["z"], 0:S], b2[:, :], Z_MIN, ALU.add, ALU.max).then_inc(zc_ready, 1)

            def silu(b, kb):
                dve.wait_ge(e_ready, b + 1)
                dve.tensor_scalar(den[:, :], e_z[:, :], 1.0, None, ALU.add).then_inc(silu_step, 1)
                dve.wait_ge(silu_step, 2 * b + 1)
                nc.vector.reciprocal(sig[:, :], den[:, :]).then_inc(silu_step, 1)
                dve.wait_ge(silu_step, 2 * b + 2)
                nc.vector.scalar_tensor_tensor(gT[:, kb % AHEAD, :], misc[:, BANK["z"], 0:S], b2[:, :], sig[:, :],
                                               ALU.add, ALU.mult).then_inc(g_ready, 1)

            def gate(b, kb):
                dve.wait_ge(s_ps, b + 1)
                if kb > 0:
                    dve.wait_ge(sgT_ps, b)
                nc.vector.scalar_tensor_tensor(sg[:, :], misc[:, BANK["proj"], 0:S], bout[:, :], gT[:, kb % AHEAD, :],
                                               ALU.add, ALU.mult).then_inc(sg_ready, 1)

            def residual(b, kb):
                dve.wait_ge(sgT_ps, b + 1)
                if kb >= 2:
                    dve.wait_ge(stored[kb % 2], 8 * (b - kb % 2))
                dve.tensor_tensor(res[:, kb % 2, :, :], xs[:, bass.ds(T * b, T), :],
                                  misc[:, BANK["back"], 0:S].rearrange("p (i d) -> p i d", i=T), ALU.add).then_inc(res_ready, 1)

            WORK = [
                (0, 0, normalise, ()), (0, 2, shift, ()), (0, 4, gate, ()), (1, 2, mT_copy, ()),
                (1, 0, qkv, (0,)), (2, 0, qkv, (1,)), (3, 4, residual, ()), (6, 2, clamp, ()), (8, 2, silu, ()),
                (8, 0, partsT_copy, (0,)), (9, 0, partsT_copy, (1,)), (10, 3, onorm_make, ()),
            ]

            def iteration(t, known):
                for step in range(STEPS):
                    for b, kb, at, _, what, args in events(WORK, t, known):
                        if at == step:
                            what(b, kb, *args)
                    if 0 <= known - 1 < B:
                        maxima(t - 1, known - 1, step)

            iterations(dve, iteration)

        @block.scalar
        def _(act):
            act.wait_ge(stat_step, 2 * NT + 1)
            nc.scalar.activation(std[:, :], mv[:, :, 1], ACT.Sqrt).then_inc(std_ready, 1)
            act.wait_ge(weights_ready, 2)

            def exponentials(b, kb, u):
                g = u // 3
                act.wait_ge(s2_ps, NU * b + u + 1)
                if kb > 0:
                    act.wait_ge(pv_ps, G * (b - 1) + g + 1)
                nc.scalar.activation(probs[:, u, :, :].rearrange("p h q -> p (h q)"), s2[:, u % 2, :], ACT.Exp,
                                     scale=SCALE).then_inc(exp_ready, 1)

            def xnT_copies(b, kb):
                src = misc[:, BANK["xnT"], 0:S]
                act.wait_ge(xnT_ps, b + 1)
                if kb >= 2:
                    act.wait_ge(qkv_ps, 2 * (b - 1))
                    act.wait_ge(xnT_lo_ready, b - 1)
                nc.scalar.copy(xnT[:, kb % 2, :], src).then_inc(xnT_ready, 1)
                if kb >= AHEAD:
                    act.wait_ge(h_ps, 2 * (b - AHEAD + 1))
                nc.scalar.copy(xnT_hi[:, kb % AHEAD, :], src).then_inc(xnT_hi_ready, 1)

            def high(b, kb):
                act.wait_ge(rotated, b + 1)
                if kb > 0:
                    act.wait_ge(partsT_ps, 2 * b)
                nc.scalar.copy(parts_flat(0), rot_flat).then_inc(part_hi, 1)

            def middle(b, kb):
                act.wait_ge(part_rem, b + 1)
                nc.scalar.copy(parts_flat(1), rem_flat).then_inc(part_mid, 1)

            rot_flat = rot[:, :, :].rearrange("p i n -> p (i n)")
            rem_flat = rem[:, :, :].rearrange("p i n -> p (i n)")

            def parts_flat(c):
                return parts[:, c, :, :, :].rearrange("p i s n -> p (i s n)")

            def hidden(b, kb, half):
                act.wait_ge(h_ps, 2 * b + half + 1)
                if kb > 0 and half == 0:
                    act.wait_ge(z_ps, b)
                for f in range(2):
                    n = 2 * half + f
                    nc.scalar.activation(hT[:, n, :], misc[:, BANK[f"h{half}"], S * f:S * (f + 1)], ACT.Relu,
                                         bias=b1[:, n:n + 1]).then_inc(h_ready, 1)

            def exp_z(b, kb):
                act.wait_ge(zc_ready, b + 1)
                if kb > 0:
                    act.wait_ge(silu_step, 2 * b)
                nc.scalar.activation(e_z[:, :], zc[:, :], ACT.Exp, scale=-1.0).then_inc(e_ready, 1)

            def oT_copy(b, kb, g):
                act.wait_ge(pv_ps, G * b + g + 1)
                if kb > 0 and g == 0:
                    act.wait_ge(o_ps, 2 * b)
                nc.scalar.copy(oT[:, g, :], pv[:, g % 2, 0:S]).then_inc(oT_ready, 1)

            def onT_copy(b, kb):
                act.wait_ge(onT_ps, b + 1)
                if kb > 0:
                    act.wait_ge(s_ps, b)
                nc.scalar.copy(onT[:, :], misc[:, BANK["onT"], 0:S]).then_inc(onT_ready, 1)

            WORK = [
                (0, 0, xnT_copies, ()), (0, 4, onT_copy, ()), (0, 3, oT_copy, (0,)), (3, 3, oT_copy, (1,)),
                (4, 2, hidden, (0,)), (5, 2, hidden, (1,)), (5, 0, high, ()), (6, 3, oT_copy, (2,)),
                (7, 2, exp_z, ()), (7, 0, middle, ()), (9, 3, oT_copy, (3,)),
            ]
            FIRST = [(0, 4, onT_copy, ())]

            def iteration(t, known):
                for step in range(STEPS):
                    for b, kb, at, _, what, args in sorted(events(WORK, t, known), key=lambda e: e[2] * 10 - (e[4] is onT_copy)):
                        if at == step:
                            what(b, kb, *args)
                    if (c := second_pass(t, known, step)) is not None:
                        exponentials(*c)

            iterations(act, iteration)

        @block.gpsimd
        def _(pool):
            pool.wait_ge(consts_loaded, 48)

            def low_x(b, kb):
                pool.wait_ge(xnT_ready, b + 1)
                pool.wait_ge(xnT_hi_ready, b + 1)
                if kb >= AHEAD:
                    pool.wait_ge(h_ps, 2 * (b - AHEAD + 1))
                pool.tensor_tensor(xnT_lo[:, kb % AHEAD, :], xnT[:, kb % 2, :], xnT_hi[:, kb % AHEAD, :],
                                   ALU.subtract).then_inc(xnT_lo_ready, 1)

            def rotate(b, kb):
                pool.wait_ge(qk_ready, 2 * b + 2)
                for i in range(T):
                    pair = lambda t, o: t[:, i, :].rearrange("p (n e) -> p n e", e=2)[:, :, o].rearrange(
                        "p (h f) -> p h f", f=DK // 2)
                    table = lambda a, n: rope[:, i, a:a + n].unsqueeze(1).broadcast_to([P, 2 * H, n])
                    if i == 0 and kb > 0:
                        pool.wait_ge(rotated, b)
                    pool.tensor_tensor(rot_a[:, i, :].rearrange("p (h d) -> p h d", d=DK),
                                       qk[:, i, :].rearrange("p (h d) -> p h d", d=DK), table(0, DK), ALU.mult
                                       ).then_inc(rope_terms, 1)
                    pool.tensor_tensor(pair(rot_b, 0), pair(qk, 1), table(8, 4), ALU.mult).then_inc(rope_terms, 1)
                    pool.tensor_tensor(pair(rot_b, 1), pair(qk, 0), table(12, 4), ALU.mult).then_inc(rope_terms, 1)
                pool.wait_ge(rope_terms, 6 * b + 6)
                if kb > 0:
                    pool.wait_ge(part_hi, b)
                    pool.wait_ge(part_rem, b)
                pool.tensor_tensor(rot_flat, rot_a[:, :, :].rearrange("p i n -> p (i n)"),
                                   rot_b[:, :, :].rearrange("p i n -> p (i n)"), ALU.add).then_inc(rotated, 1)

            rot_flat = rot[:, :, :].rearrange("p i n -> p (i n)")
            rem_flat = rem[:, :, :].rearrange("p i n -> p (i n)")

            def parts_flat(c):
                return parts[:, c, :, :, :].rearrange("p i s n -> p (i s n)")

            def remainder(b, kb):
                pool.wait_ge(part_hi, b + 1)
                pool.wait_ge(rotated, b + 1)
                if kb > 0:
                    pool.wait_ge(part_lo, b)
                    pool.wait_ge(part_mid, b)
                pool.tensor_tensor(rem_flat, rot_flat, parts_flat(0), ALU.subtract).then_inc(part_rem, 1)

            def low(b, kb):
                pool.wait_ge(part_mid, b + 1)
                pool.wait_ge(part_rem, b + 1)
                pool.tensor_tensor(parts_flat(2), rem_flat, parts_flat(1), ALU.subtract).then_inc(part_lo, 1)

            def causal(b, kb, u):
                if UNITS[u][1] != UNITS[u][2]:
                    return
                pool.wait_ge(exp_ready, NU * b + u + 1)
                pool.sem_inc(exp_seen, 1)
                nc.gpsimd.affine_select(out=probs[:, u, :, :], in_=probs[:, u, :, :], pattern=[[0, 4], [1, P]],
                                        compare_op=ALU.is_ge, fill=0.0, base=0, channel_multiplier=-1
                                        ).then_inc(causal_ready, 1)

            WORK = [(1, 0, low_x, ()), (2, 0, rotate, ()), (6, 0, remainder, ()), (7, 0, low, ())]

            def iteration(t, known):
                for step in range(STEPS):
                    for b, kb, at, _, what, args in events(WORK, t, known):
                        if at == step:
                            what(b, kb, *args)
                    if (c := second_pass(t, known, step)) is not None:
                        causal(*c)

            iterations(pool, iteration)


def kernel(L0_attn_x, L0_attn_w_qkv, L0_attn_b_qkv, L0_attn_w_out, L0_attn_b_out, L0_ffn_W1, L0_ffn_b1,
           L0_ffn_W2, L0_ffn_b2):
    import numpy as np
    import concourse.bacc as bacc
    from concourse.bass_utils import run_bass_kernel_spmd

    x = np.ascontiguousarray(L0_attn_x)
    B, S, D = x.shape
    F = L0_ffn_W1.shape[0]
    tall = np.ascontiguousarray
    ident = np.eye(P, dtype=np.float32)
    mask = np.where(np.arange(P)[None, :] > np.arange(P)[:, None], np.float32(MASKED), np.float32(0))
    freq = np.float32(10000.0) ** (-np.arange(0, DK, 2, dtype=np.float32) / np.float32(DK))
    angle = np.arange(S, dtype=np.float32)[:, None] * freq[None, :]
    cos, sin = np.cos(angle), np.sin(angle)
    rope = np.concatenate([np.repeat(cos, 2, axis=1), -sin, sin], axis=1).reshape(S // P, P, 16).transpose(1, 0, 2)
    arrays = {
        "x": x,
        "w_qkv_t": tall(np.asarray(L0_attn_w_qkv).T),
        "b_qkv_all": tall(np.broadcast_to(np.asarray(L0_attn_b_qkv)[None, :], (P, 3 * D))),
        "w_out_t": tall(np.asarray(L0_attn_w_out).T),
        "b_out_col": tall(np.asarray(L0_attn_b_out)[:, None]),
        "w1_t": tall(np.asarray(L0_ffn_W1).T),
        "w1_rows": tall(np.asarray(L0_ffn_W1).reshape(F // P, P, D).transpose(1, 0, 2)),
        "b1_cols": tall(np.asarray(L0_ffn_b1).reshape(F // P, P).T),
        "w2_t": tall(np.asarray(L0_ffn_W2).T.reshape(F // P, P, D).transpose(1, 0, 2)),
        "w2_rows": tall(np.asarray(L0_ffn_W2)),
        "b2_col": tall(np.asarray(L0_ffn_b2)[:, None]),
        "ident_in": ident, "mask_in": tall(mask), "rope_in": tall(rope),
    }
    nc = bacc.Bacc("TRN2", target_bir_lowering=False, num_devices=1)
    args = [nc.dram_tensor(n, a.shape, mybir.dt.from_np(a.dtype), kind="ExternalInput").ap() for n, a in arrays.items()]
    args.append(nc.dram_tensor("y", x.shape, F32, kind="ExternalOutput").ap())
    attention_ffn_gate(nc, *args)
    return run_bass_kernel_spmd(nc, [arrays], core_ids=[0]).results[0]["y"]
```

```python
from contextlib import ExitStack

import concourse.bass as bass
from concourse import mybir

F32 = mybir.dt.float32
BF16 = mybir.dt.bfloat16
F16 = mybir.dt.float16
ALU = mybir.AluOpType
ACT = mybir.ActivationFunctionType
AX_X = mybir.AxisListType.X

P = 128
DK = 8
QUAD = 32
LN_EPS = 1e-5
Q_EPS = 1e-5
SUM_EPS = 1e-8
MASKED = -1e30
PARTS = 3
ROWS = DK * PARTS * PARTS
SHIFT_ROWS = ROWS + PARTS
AHEAD = 4

STEPS = 12
PASS1 = 16
PASS2 = 33


def attention_ffn_gate(nc, x, w_qkv_t, b_qkv_all, w_out_t, b_out_col, w1_t, w1_rows, b1_cols,
                       w2_t, w2_rows, b2_col, ident_in, mask_in, rope_in, out):
    B, S, D = x.shape
    T = S // P
    H = D // DK
    F = w1_t.shape[1]
    FB = F // P
    G = H // 4
    SCALE = float(DK) ** -0.5
    NT = B * T
    HEADW = DK + 1
    assert T == 2 and D == P and G == 4 and FB == 4 and 3 * G == STEPS

    UNITS = [(g, kb, qb) for g in range(G) for kb, qb in ((0, 0), (0, 1), (1, 1))]
    NU = len(UNITS)

    with ExitStack() as ctx:
        def sb(name, shape, dt=F32):
            return ctx.enter_context(nc.sbuf_tensor(name, shape, dt))

        def sem(name):
            return ctx.enter_context(nc.semaphore(name))

        ident = sb("ident", [P, P])
        ident_bf = sb("ident_bf", [P, P], BF16)
        mask = sb("mask", [P, P])
        mask_bf = sb("mask_bf", [P, P], BF16)
        rope = sb("rope", [P, T, 4 * DK])
        ones = sb("ones", [P, P])
        wqkv = sb("wqkv", [P, 3 * D])
        bqkv = sb("bqkv", [P, 3 * D])
        wout = sb("wout", [P, D])
        bout = sb("bout", [P, 1])
        w1 = sb("w1", [P, F])
        w1n = sb("w1n", [P, FB, D])
        w2 = sb("w2", [P, FB, D])
        w2n = sb("w2n", [P, F])
        b1 = sb("b1", [P, FB])
        b2 = sb("b2", [P, 1])
        wabs = sb("wabs", [P, 2])
        gam = sb("gam", [P, 2])
        thr = sb("thr", [P, 2, 2])
        lowq = sb("lowq", [P, 2, F])
        w1q = sb("w1q", [P, F], F16)
        w2q = sb("w2q", [P, FB, D])
        xs = sb("xs", [P, NT, D])
        stats = sb("stats", [P, NT, 6])
        mv = sb("mv", [P, NT, 2])
        std = sb("std", [P, NT])
        rstd = sb("rstd", [P, NT])
        xn = sb("xn", [P, T, D])
        xnT = sb("xnT", [P, 2, S])
        xnT_hi = sb("xnT_hi", [P, AHEAD, S], F16)
        xnT_lo = sb("xnT_lo", [P, AHEAD, S], F16)
        qk = sb("qk", [P, T, 2 * D])
        vaug = sb("vaug", [P, AHEAD, T, H, HEADW])
        rot_a = sb("rot_a", [P, T, 2 * D])
        rot_b = sb("rot_b", [P, T, 2 * D])
        rot = sb("rot", [P, T, 2 * D])
        rem = sb("rem", [P, T, 2 * D])
        parts = sb("parts", [P, PARTS, T, 2, D], BF16)
        partsT = sb("partsT", [P, 2, PARTS, S], BF16)
        qstack = sb("qstack", [P, AHEAD, H, S], BF16)
        kstack = sb("kstack", [P, AHEAD, H, S], BF16)
        mx = sb("mx", [P, 2, 3, H])
        mrem = sb("mrem", [P, T, H])
        mparts = sb("mparts", [P, T, P // H, H], BF16)
        mT = sb("mT", [PARTS * H, S], BF16)
        probs = sb("probs", [P, NU, 4, P])
        oT = sb("oT", [P, G, S])
        lsum = sb("lsum", [P, T, H])
        linv = sb("linv", [P, T, H])
        onorm = sb("onorm", [P, T, D])
        onT = sb("onT", [P, S])
        hT = sb("hT", [P, FB, S])
        zh = sb("zh", [P, S])
        th = sb("th", [P, S])
        gT = sb("gT", [P, AHEAD, S])
        sg = sb("sg", [P, S])
        res = sb("res", [P, 2, T, D])

        s1 = ctx.enter_context(nc.psum_tensor("s1", [P, 2, 512], F32))
        s2 = ctx.enter_context(nc.psum_tensor("s2", [P, 2, 512], F32))
        pv = ctx.enter_context(nc.psum_tensor("pv", [P, 2, 512], F32))
        misc = ctx.enter_context(nc.psum_tensor("misc", [P, 2, 512], F32))

        x_loaded = [sem(f"x_loaded{i}") for i in range(2)]
        consts_loaded = sem("consts_loaded")
        weights_loaded = sem("weights_loaded")
        spread_out = [sem(f"spread_out{i}") for i in range(2)]
        stacks_loaded = [sem(f"stacks_loaded{i}") for i in range(2)]
        shifts_loaded = sem("shifts_loaded")
        stored = [sem(f"stored{i}") for i in range(2)]
        stack_ones = sem("stack_ones")
        consts_ready = sem("consts_ready")
        abs_ready = sem("abs_ready")
        gamma_sum = sem("gamma_sum")
        quant_step = sem("quant_step")
        weights_ready = sem("weights_ready")
        pv_zeroed = sem("pv_zeroed")
        stat_step = sem("stat_step")
        std_ready = sem("std_ready")
        rstd_ready = sem("rstd_ready")
        xn_ready = sem("xn_ready")
        xnT_ps = sem("xnT_ps")
        xnT_ready = sem("xnT_ready")
        xnT_hi_ready = sem("xnT_hi_ready")
        xnT_lo_ready = sem("xnT_lo_ready")
        qkv_ps = sem("qkv_ps")
        qk_ready = sem("qk_ready")
        v_ready = sem("v_ready")
        v_ones = sem("v_ones")
        mmax_ready = sem("mmax_ready")
        rope_terms = sem("rope_terms")
        rotated = sem("rotated")
        part_hi = sem("part_hi")
        part_rem = sem("part_rem")
        part_mid = sem("part_mid")
        part_lo = sem("part_lo")
        partsT_ps = sem("partsT_ps")
        partsT_ready = sem("partsT_ready")
        s1_ps = sem("s1_ps")
        max_ready = sem("max_ready")
        shift_step = sem("shift_step")
        mT_ps = sem("mT_ps")
        mT_ready = sem("mT_ready")
        s2_ps = sem("s2_ps")
        exp_ready = sem("exp_ready")
        exp_seen = sem("exp_seen")
        causal_ready = sem("causal_ready")
        pv_ps = sem("pv_ps")
        oT_ready = sem("oT_ready")
        o_ps = sem("o_ps")
        sum_ready = sem("sum_ready")
        onorm_ready = sem("onorm_ready")
        onT_ps = sem("onT_ps")
        onT_ready = sem("onT_ready")
        h_ps = sem("h_ps")
        h_ready = sem("h_ready")
        z_ps = sem("z_ps")
        zh_ready = sem("zh_ready")
        tanh_ready = sem("tanh_ready")
        g_ready = sem("g_ready")
        s_ps = sem("s_ps")
        sg_ready = sem("sg_ready")
        sgT_ps = sem("sgT_ps")
        res_ready = sem("res_ready")

        JOBS = [
            (0, "xnT", [(xnT_ready, 1, 1), (xnT_hi_ready, 1, 1)]),
            (1, "qkv0", [(qk_ready, 2, 1), (v_ready, 2, 1)]),
            (49, "o0", [(onorm_ready, 1, 1)]),
            (49, "o1", [(onorm_ready, 1, 1)]),
            (51, "onT", [(onT_ready, 1, 1)]),
            (3, "qkv1", [(qk_ready, 2, 2), (v_ready, 2, 2)]),
            (52, "proj", [(sg_ready, 1, 1)]),
            (40, "h1", [(h_ready, FB, 4)]),
            (29, "shift", [(mT_ready, 1, 1)]),
            (54, "back", [(res_ready, 1, 1)]),
            (42, "z", [(zh_ready, 1, 1)]),
            (33, "h0", [(h_ready, FB, 2)]),
            (10, "partsq", [(partsT_ready, 2, 1)]),
            (10, "partsk", [(partsT_ready, 2, 2)]),
        ]
        assert all(a[0] % STEPS <= b[0] % STEPS for a, b in zip(JOBS, JOBS[1:]))
        BANK = {name: n % 2 for n, (_, name, _) in enumerate(JOBS)}
        assert (BANK["o0"], BANK["o1"]) == (0, 1)
        NJ = len(JOBS)

        def at_step(table, step, t, known):
            for row in table:
                lag = row[0] // STEPS
                if row[0] % STEPS == step and 0 <= known - lag < B:
                    yield t - lag, known - lag, row

        def iterations(eng, body):
            for t in range(AHEAD):
                body(t, t)
            with eng.Fori(AHEAD, B - AHEAD + 1, AHEAD) as t0:
                for j in range(AHEAD):
                    body(t0 + j, AHEAD + j)
            for t in range(B, B + AHEAD):
                body(t, t)

        FIRST_PASS = [(PASS1 + u, u) for u in range(NU)]
        SECOND_PASS = [(PASS2 + u, u) for u in range(NU)]

        scratch = nc.dram_tensor("scratch", [2, 2, PARTS, D, S], BF16, kind="Internal").ap()

        block = ctx.enter_context(nc.Block())

        @block.sync
        def _(sp):
            half = NT // 2
            xt = x.rearrange("b (i p) d -> p (b i) d", p=P)
            sp.dma_start(xs[:, 0:half, :], xt[:, 0:half, :]).then_inc(x_loaded[0], 16)
            for dst, src in ((ident, ident_in), (mask, mask_in), (rope, rope_in)):
                sp.dma_start(dst[:], src).then_inc(consts_loaded, 16)
            for dst, src in ((wqkv, w_qkv_t), (bqkv, b_qkv_all), (wout, w_out_t), (bout, b_out_col),
                             (w1, w1_t), (w1n, w1_rows), (w2, w2_t), (w2n, w2_rows), (b1, b1_cols),
                             (b2, b2_col)):
                sp.dma_start(dst[:], src).then_inc(weights_loaded, 16)
            sp.dma_start(xs[:, half:NT, :], xt[:, half:NT, :]).then_inc(x_loaded[1], 16)
            sp.wait_ge(stack_ones, 1)

            def spread(b, kb, side):
                sp.wait_ge(partsT_ready, 2 * b + side + 1)
                sp.dma_start(scratch[kb % 2, side].rearrange("c p s -> p c s"), partsT[:, side, :, :]
                             ).then_inc(spread_out[side], 16)

            def stack(b, kb, side):
                sp.wait_ge(spread_out[side], 16 * (b + 1))
                if side == 0:
                    src = scratch[kb % 2, 0].rearrange("c (d h) s -> (c d) (h s)", d=DK)
                    sp.dma_start(qstack[0:ROWS, kb % AHEAD, :, :].rearrange("p h s -> p (h s)"),
                                 src.unsqueeze(1).broadcast_to([PARTS * DK, PARTS, H * S])
                                 ).then_inc(stacks_loaded[kb % 2], 16)
                    return
                for n in range(PARTS):
                    rows = slice(DK * PARTS * n, DK * PARTS * (n + 1))
                    sp.dma_start(kstack[rows, kb % AHEAD, :, :].rearrange("p h s -> p (h s)"),
                                 scratch[kb % 2, 1].rearrange("c (d h) s -> d c (h s)", d=DK)
                                 ).then_inc(stacks_loaded[kb % 2], 16)

            def shift(b, kb):
                sp.wait_ge(mT_ready, b + 1)
                for c in range(PARTS):
                    sp.dma_start(qstack[ROWS + c:ROWS + c + 1, kb % AHEAD, :, :],
                                 mT[H * c:H * (c + 1), :]).then_inc(shifts_loaded, 16)

            def store(b, kb):
                sp.wait_ge(res_ready, b + 1)
                sp.dma_start(out[bass.ds(b, 1), :, :].rearrange("o (i p) d -> p (o i) d", p=P),
                             res[:, kb % 2, :, :]).then_inc(stored[kb % 2], 16)

            WORK = [(29, shift), (55, store), (10, spread, 0), (11, spread, 1), (11, stack, 0), (11, stack, 1)]

            def iteration(t, known):
                for step in range(STEPS):
                    for b, kb, (_, what, *args) in at_step(WORK, step, t, known):
                        what(b, kb, *args)

            iterations(sp, iteration)
            for s in stored:
                sp.wait_ge(s, 16 * B // 2)

        @block.tensor
        def _(pe):
            pe.wait_ge(abs_ready, 3)
            nc.tensor.matmul(misc[:, 0, 0:2], ones[:, :], wabs[:, :], start=True, stop=True).then_inc(gamma_sum, 1)
            pe.wait_ge(weights_ready, 2)
            pe.wait_ge(consts_ready, 2)
            pe.wait_ge(pv_zeroed, 1)
            pe.wait_ge(weights_loaded, 160)

            def job_bank(n, t, known):
                for back in range(2, 4 * NJ, 2):
                    m, it = (n - back) % NJ, (n - back) // NJ
                    lag = JOBS[m][0] // STEPS
                    if 0 <= known + it - lag < B:
                        for s, per, at in JOBS[m][2]:
                            pe.wait_ge(s, per * (t + it - lag) + at)
                        return

            def job(n, t, known, name, b, kb):
                bank = misc[:, BANK[name], :]
                job_bank(n, t, known)
                buf = kb % AHEAD
                if name == "xnT":
                    pe.wait_ge(xn_ready, 2 * b + 2)
                    for i in range(T):
                        mm = nc.tensor.transpose(bank[:, P * i:P * (i + 1)], xn[:, i, :], ident[:, :])
                    mm.then_inc(xnT_ps, 1)
                elif name in ("qkv0", "qkv1"):
                    i = int(name[-1])
                    pe.wait_ge(xnT_ready, b + 1)
                    nc.tensor.matmul(bank[:, 0:3 * D], xnT[:, kb % 2, P * i:P * (i + 1)], wqkv[:, :],
                                     start=True, stop=True).then_inc(qkv_ps, 1)
                elif name in ("partsq", "partsk"):
                    side = name == "partsk"
                    pe.wait_ge(part_lo, b + 1)
                    dst = bank.bitcast(BF16).rearrange("p (c s) -> p c s", s=S)
                    for c in range(PARTS):
                        for i in range(T):
                            mm = nc.tensor.transpose(dst[:, c, P * i:P * (i + 1)], parts[:, c, i, int(side), :],
                                                     ident_bf[:, :])
                    mm.then_inc(partsT_ps, 1)
                elif name == "shift":
                    pe.wait_ge(shift_step, 4 * b + 4)
                    dst = bank.bitcast(BF16)
                    for i in range(T):
                        mm = nc.tensor.transpose(dst[:, P * i:P * (i + 1)],
                                                 mparts[:, i, :, :].rearrange("p c h -> p (c h)"), ident_bf[:, :])
                    mm.then_inc(mT_ps, 1)
                elif name in ("h0", "h1"):
                    pe.wait_ge(xnT_lo_ready, b + 1)
                    pe.wait_ge(xnT_hi_ready, b + 1)
                    for f in range(2):
                        w = w1q[:, P * (2 * int(name[-1]) + f):P * (2 * int(name[-1]) + f + 1)]
                        for k, part in enumerate((xnT_hi, xnT_lo)):
                            mm = nc.tensor.matmul(bank[:, S * f:S * (f + 1)], w, part[:, buf, :],
                                                  start=k == 0, stop=k == 1)
                    mm.then_inc(h_ps, 1)
                elif name == "z":
                    pe.wait_ge(h_ready, FB * b + FB)
                    for f in range(FB // 2):
                        nc.tensor.matmul(bank[:, 0:S], w2q[:, f, :], hT[:, f, :], start=f == 0, stop=False)
                elif name in ("o0", "o1"):
                    i = int(name[-1])
                    pe.wait_ge(oT_ready, G * b + G)
                    for g in range(G):
                        mm = nc.tensor.transpose(bank[:, P * g:P * (g + 1)], oT[:, g, P * i:P * (i + 1)], ident[:, :])
                    mm.then_inc(o_ps, 1)
                elif name == "onT":
                    pe.wait_ge(onorm_ready, b + 1)
                    for i in range(T):
                        mm = nc.tensor.transpose(bank[:, P * i:P * (i + 1)], onorm[:, i, :], ident[:, :])
                    mm.then_inc(onT_ps, 1)
                elif name == "proj":
                    pe.wait_ge(onT_ready, b + 1)
                    nc.tensor.matmul(bank[:, 0:S], wout[:, :], onT[:, :], start=True, stop=True).then_inc(s_ps, 1)
                elif name == "back":
                    pe.wait_ge(sg_ready, b + 1)
                    for i in range(T):
                        mm = nc.tensor.transpose(bank[:, P * i:P * (i + 1)], sg[:, P * i:P * (i + 1)], ident[:, :])
                    mm.then_inc(sgT_ps, 1)

            def z_rest(b, kb):
                for f in range(FB // 2, FB):
                    mm = nc.tensor.matmul(misc[:, BANK["z"], 0:S], w2q[:, f, :], hT[:, f, :], start=False, stop=f == FB - 1)
                mm.then_inc(z_ps, 1)

            def pass1(b, kb, u):
                g, key, query = UNITS[u]
                if u == 0:
                    pe.wait_ge(stacks_loaded[kb % 2], 16 * (1 + PARTS) // 2 * (b - kb % 2) + 16 * (1 + PARTS))
                if kb > 0 or u >= 2:
                    pe.wait_ge(max_ready, NU * b + u - 1)
                bank = s1[:, u % 2, :]
                diagonal = key == query
                if diagonal:
                    nc.tensor.matmul(bank.rearrange("p (h k) -> p h k", h=4), ident_bf[:, :],
                                     mask_bf[:, :].unsqueeze(1).broadcast_to([P, 4, P]), start=True, stop=False)
                for j in range(4):
                    h = 4 * g + j
                    mm = nc.tensor.matmul(bank[:, P * j:P * (j + 1)],
                                          qstack[0:ROWS, kb % AHEAD, h, P * query:P * (query + 1)],
                                          kstack[0:ROWS, kb % AHEAD, h, P * key:P * (key + 1)],
                                          start=not diagonal, stop=not diagonal or j == 3)
                mm.then_inc(s1_ps, 1)

            def pass2(b, kb, u):
                g, key, query = UNITS[u]
                if u == 0:
                    pe.wait_ge(shifts_loaded, 16 * PARTS * (b + 1))
                if kb > 0 or u >= 2:
                    pe.wait_ge(exp_ready, NU * b + u - 1)
                for j in range(4):
                    h = 4 * g + j
                    mm = nc.tensor.matmul(s2[:, u % 2, P * j:P * (j + 1)],
                                          kstack[0:SHIFT_ROWS, kb % AHEAD, h, P * key:P * (key + 1)],
                                          qstack[0:SHIFT_ROWS, kb % AHEAD, h, P * query:P * (query + 1)],
                                          start=True, stop=True)
                mm.then_inc(s2_ps, 1)

            def weigh(b, kb, g):
                pe.wait_ge(causal_ready, 2 * G * b + 2 * g + 2)
                pe.wait_ge(exp_ready, NU * b + 3 * g + 3)
                pe.wait_ge(v_ready, 2 * b + 2)
                if kb > 0 or g >= 2:
                    pe.wait_ge(oT_ready, G * b + g - 1)
                for j in range(4):
                    nc.tensor.matmul(pv[QUAD * j:QUAD * j + HEADW, g % 2, 0:S], vaug[:, kb % AHEAD, 0, 4 * g + j, :],
                                     probs[:, 3 * g:3 * g + 2, j, :], start=True, stop=False)
                for j in range(4):
                    mm = nc.tensor.matmul(pv[QUAD * j:QUAD * j + HEADW, g % 2, P:S], vaug[:, kb % AHEAD, 1, 4 * g + j, :],
                                          probs[:, 3 * g + 2, j, :], start=False, stop=True)
                mm.then_inc(pv_ps, 1)

            WEIGH = [(PASS2 + 3 * g + 5, weigh, g) for g in range(G)] + [(43, z_rest)]

            def iteration(t, known):
                for step in range(STEPS):
                    for b, kb, (_, u) in at_step(FIRST_PASS, step, t, known):
                        pass1(b, kb, u)
                    for b, kb, (_, u) in at_step(SECOND_PASS, step, t, known):
                        pass2(b, kb, u)
                    for b, kb, row in at_step(JOBS, step, t, known):
                        job(JOBS.index(row), t, known, row[1], b, kb)
                    for b, kb, (_, what, *args) in at_step(WEIGH, step, t, known):
                        what(b, kb, *args)

            iterations(pe, iteration)

        @block.vector
        def _(dve):
            dve.memset(ones[:, :], 1.0).then_inc(abs_ready, 1)
            dve.memset(kstack[64:96, :, :, :], 1.0).then_inc(stack_ones, 1)
            dve.memset(vaug[:, :, :, :, DK:HEADW], 1.0).then_inc(v_ones, 1)
            dve.memset(pv[:, :, :], 0.0).then_inc(pv_zeroed, 1)
            dve.memset(mparts[:, :, :, :], 0.0).then_inc(mmax_ready, 1)
            dve.wait_ge(consts_loaded, 48)
            dve.tensor_copy(ident_bf[:, :], ident[:, :]).then_inc(consts_ready, 1)
            dve.tensor_copy(mask_bf[:, :], mask[:, :]).then_inc(consts_ready, 1)
            dve.wait_ge(weights_loaded, 160)
            nc.vector.tensor_reduce(wabs[:, 0:1], w1n[:, :, :], axis=mybir.AxisListType.XY, op=ALU.add,
                                    apply_absolute_value=True).then_inc(abs_ready, 1)
            nc.vector.tensor_reduce(wabs[:, 1:2], w2n[:, :], axis=AX_X, op=ALU.add,
                                    apply_absolute_value=True).then_inc(abs_ready, 1)
            dve.wait_ge(gamma_sum, 1)
            dve.tensor_scalar(gam[:, :], misc[:, 0, 0:2], 1.0 / (F * D), Q_EPS, ALU.mult, ALU.add).then_inc(quant_step, 1)
            dve.wait_ge(quant_step, 1)
            dve.tensor_scalar(thr[:, 0, :], gam[:, :], 0.5, None, ALU.mult).then_inc(quant_step, 1)
            dve.tensor_scalar(thr[:, 1, :], gam[:, :], -0.5, None, ALU.mult).then_inc(quant_step, 1)
            dve.wait_ge(quant_step, 3)
            w2flat = w2[:, :, :].rearrange("p f d -> p (f d)")
            w2qflat = w2q[:, :, :].rearrange("p f d -> p (f d)")
            for n, (w, q) in enumerate(((w1[:, :], w1q[:, :]), (w2flat, w2qflat))):
                dve.tensor_scalar(lowq[:, n, :], w, thr[:, 1, n:n + 1], None, ALU.is_lt).then_inc(quant_step, 1)
                dve.wait_ge(quant_step, 4 + n)
                nc.vector.scalar_tensor_tensor(q, w, thr[:, 0, n:n + 1], lowq[:, n, :], ALU.is_gt,
                                               ALU.subtract).then_inc(weights_ready, 1)
            for tile in range(NT):
                if tile % (NT // 2) == 0:
                    dve.wait_ge(x_loaded[tile // (NT // 2)], 16)
                nc.vector.bn_stats(stats[:, tile, :], xs[:, tile, :]).then_inc(stat_step, 1)
            dve.wait_ge(stat_step, NT)
            for tile in range(NT):
                nc.vector.bn_aggr(mv[:, tile, :], stats[:, tile, :]).then_inc(stat_step, 1)
            dve.wait_ge(stat_step, 2 * NT)
            dve.tensor_scalar(mv[:, :, 1], mv[:, :, 1], LN_EPS, None, ALU.add).then_inc(stat_step, 1)
            dve.wait_ge(std_ready, 1)
            nc.vector.reciprocal(rstd[:, :], std[:, :]).then_inc(rstd_ready, 1)
            dve.wait_ge(rstd_ready, 1)
            dve.wait_ge(v_ones, 1)

            def maxima(b, kb, u):
                g, key, query = UNITS[u]
                dve.wait_ge(s1_ps, NU * b + u + 1)
                if u == 0 and kb > 1:
                    dve.wait_ge(shift_step, 4 * (b - 1))
                slot = {(0, 0): 0, (1, 1): 1, (0, 1): 2}[(key, query)]
                nc.vector.tensor_reduce(mx[:, kb % 2, slot, 4 * g:4 * g + 4], s1[:, u % 2, :].rearrange("p (h k) -> p h k", h=4),
                                        axis=AX_X, op=ALU.max).then_inc(max_ready, 1)

            def normalise(b, kb):
                if kb > 0:
                    dve.wait_ge(xnT_ps, b)
                for i in range(T):
                    tile = T * b + i
                    ti = bass.ds(tile, 1)
                    dve.tensor_scalar(xn[:, i:i + 1, :], xs[:, ti, :], mv_of(tile), rstd_of(tile),
                                      ALU.subtract, ALU.mult).then_inc(xn_ready, 1)

            def mv_of(tile):
                return mv[:, bass.ds(tile, 1), 0]

            def rstd_of(tile):
                return rstd[:, bass.ds(tile, 1)]

            def qkv(b, kb, i):
                dve.wait_ge(qkv_ps, 2 * b + i + 1)
                if kb > 0:
                    dve.wait_ge(part_lo, b)
                bank = misc[:, BANK[f"qkv{i}"], :]
                dve.tensor_tensor(qk[:, i, :], bank[:, 0:2 * D], bqkv[:, 0:2 * D], ALU.add).then_inc(qk_ready, 1)
                if kb >= AHEAD:
                    dve.wait_ge(pv_ps, G * (b - AHEAD + 1))
                dve.tensor_tensor(vaug[:, kb % AHEAD, i, :, 0:DK],
                                  bank[:, 2 * D:3 * D].rearrange("p (h d) -> p h d", d=DK),
                                  bqkv[:, 2 * D:3 * D].rearrange("p (h d) -> p h d", d=DK), ALU.add).then_inc(v_ready, 1)

            def partsT_copy(b, kb, side):
                dve.wait_ge(partsT_ps, 2 * b + side + 1)
                if kb > 0:
                    dve.wait_ge(spread_out[side], 16 * b)
                name = ("partsq", "partsk")[side]
                dve.tensor_copy(partsT[:, side, :, :],
                                misc[:, BANK[name], :].bitcast(BF16)[:, 0:PARTS * S].rearrange("p (c s) -> p c s", c=PARTS)
                                ).then_inc(partsT_ready, 1)

            def shift(b, kb):
                dve.wait_ge(max_ready, NU * b + NU)
                if kb > 0:
                    dve.wait_ge(mT_ps, b)
                dve.tensor_tensor(mx[:, kb % 2, 1, :], mx[:, kb % 2, 1, :], mx[:, kb % 2, 2, :], ALU.max).then_inc(mmax_ready, 1)
                dve.wait_ge(mmax_ready, b + 2)
                m = mx[:, kb % 2, 0:2, :]
                dve.tensor_scalar(mparts[:, :, 0, :], m, -1.0, None, ALU.mult).then_inc(shift_step, 1)
                dve.wait_ge(shift_step, 4 * b + 1)
                nc.vector.scalar_tensor_tensor(mrem[:, :, :], m, -1.0, mparts[:, :, 0, :], ALU.mult,
                                               ALU.subtract).then_inc(shift_step, 1)
                dve.wait_ge(shift_step, 4 * b + 2)
                dve.tensor_copy(mparts[:, :, 1, :], mrem[:, :, :]).then_inc(shift_step, 1)
                dve.wait_ge(shift_step, 4 * b + 3)
                dve.tensor_tensor(mparts[:, :, 2, :], mrem[:, :, :], mparts[:, :, 1, :], ALU.subtract).then_inc(shift_step, 1)

            def mT_copy(b, kb):
                dve.wait_ge(mT_ps, b + 1)
                if kb > 0:
                    dve.wait_ge(shifts_loaded, 16 * PARTS * b)
                dve.tensor_copy(mT[:, :], misc[0:PARTS * H, BANK["shift"], :].bitcast(BF16)[:, 0:S]).then_inc(mT_ready, 1)

            def onorm_make(b, kb):
                dve.wait_ge(o_ps, 2 * b + 2)
                heads = misc[:, :, :].rearrange("p i (h w) -> p i h w", w=QUAD)
                if kb > 0:
                    dve.wait_ge(onT_ps, b)
                dve.tensor_scalar(lsum[:, :, :], heads[:, :, :, DK], SUM_EPS, None, ALU.add).then_inc(sum_ready, 1)
                dve.wait_ge(sum_ready, 2 * b + 1)
                nc.vector.reciprocal(linv[:, :, :], lsum[:, :, :]).then_inc(sum_ready, 1)
                dve.wait_ge(sum_ready, 2 * b + 2)
                dve.tensor_tensor(onorm[:, :, :].rearrange("p i (h d) -> p (i h) d", d=DK),
                                  heads[:, :, :, 0:DK].rearrange("p i h d -> p (i h) d"),
                                  linv[:, :, :].rearrange("p i h -> p (i h)").unsqueeze(2).broadcast_to([P, T * H, DK]),
                                  ALU.mult).then_inc(onorm_ready, 1)

            def half_z(b, kb):
                dve.wait_ge(z_ps, b + 1)
                dve.tensor_scalar(zh[:, :], misc[:, BANK["z"], 0:S], b2[:, :], 0.5, ALU.add, ALU.mult).then_inc(zh_ready, 1)

            def silu(b, kb):
                dve.wait_ge(zh_ready, b + 1)
                dve.wait_ge(tanh_ready, b + 1)
                nc.vector.scalar_tensor_tensor(gT[:, kb % AHEAD, :], th[:, :], 1.0, zh[:, :],
                                               ALU.add, ALU.mult).then_inc(g_ready, 1)

            def gate(b, kb):
                dve.wait_ge(s_ps, b + 1)
                if kb > 0:
                    dve.wait_ge(sgT_ps, b)
                nc.vector.scalar_tensor_tensor(sg[:, :], misc[:, BANK["proj"], 0:S], bout[:, :], gT[:, kb % AHEAD, :],
                                               ALU.add, ALU.mult).then_inc(sg_ready, 1)

            def residual(b, kb):
                dve.wait_ge(sgT_ps, b + 1)
                if kb >= 2:
                    dve.wait_ge(stored[kb % 2], 8 * (b - kb % 2))
                dve.tensor_tensor(res[:, kb % 2, :, :], xs[:, bass.ds(T * b, T), :],
                                  misc[:, BANK["back"], 0:S].rearrange("p (i d) -> p i d", i=T), ALU.add).then_inc(res_ready, 1)

            WORK = [
                (0, normalise), (1, qkv, 0), (50, onorm_make), (3, qkv, 1), (53, gate), (28, shift), (29, mT_copy),
                (54, residual), (43, half_z), (44, silu), (10, partsT_copy, 0), (11, partsT_copy, 1),
            ]

            def iteration(t, known):
                for step in range(STEPS):
                    for b, kb, (_, u) in at_step(FIRST_PASS, step, t, known):
                        maxima(b, kb, u)
                    for b, kb, (_, what, *args) in at_step(WORK, step, t, known):
                        what(b, kb, *args)

            iterations(dve, iteration)

        @block.scalar
        def _(act):
            act.wait_ge(stat_step, 2 * NT + 1)
            nc.scalar.activation(std[:, :], mv[:, :, 1], ACT.Sqrt).then_inc(std_ready, 1)
            act.wait_ge(weights_ready, 2)

            def exponentials(b, kb, u):
                g = u // 3
                act.wait_ge(s2_ps, NU * b + u + 1)
                if kb > 0:
                    act.wait_ge(pv_ps, G * (b - 1) + g + 1)
                nc.scalar.activation(probs[:, u, :, :].rearrange("p h q -> p (h q)"), s2[:, u % 2, :], ACT.Exp,
                                     scale=SCALE).then_inc(exp_ready, 1)

            def xnT_copies(b, kb):
                src = misc[:, BANK["xnT"], 0:S]
                act.wait_ge(xnT_ps, b + 1)
                if kb >= 2:
                    act.wait_ge(qkv_ps, 2 * (b - 1))
                    act.wait_ge(xnT_lo_ready, b - 1)
                nc.scalar.copy(xnT[:, kb % 2, :], src).then_inc(xnT_ready, 1)
                if kb >= AHEAD:
                    act.wait_ge(h_ps, 2 * (b - AHEAD + 1))
                nc.scalar.copy(xnT_hi[:, kb % AHEAD, :], src).then_inc(xnT_hi_ready, 1)

            def high(b, kb):
                act.wait_ge(rotated, 2 * b + 2)
                if kb > 0:
                    act.wait_ge(partsT_ps, 2 * b)
                nc.scalar.copy(parts_flat(0), rot_flat).then_inc(part_hi, 1)

            def middle(b, kb):
                act.wait_ge(part_rem, b + 1)
                nc.scalar.copy(parts_flat(1), rem_flat).then_inc(part_mid, 1)

            rot_flat = rot[:, :, :].rearrange("p i n -> p (i n)")
            rem_flat = rem[:, :, :].rearrange("p i n -> p (i n)")

            def parts_flat(c):
                return parts[:, c, :, :, :].rearrange("p i s n -> p (i s n)")

            def hidden(b, kb, half):
                act.wait_ge(h_ps, 2 * b + half + 1)
                if kb > 0 and half == 0:
                    act.wait_ge(z_ps, b)
                for f in range(2):
                    n = 2 * half + f
                    nc.scalar.activation(hT[:, n, :], misc[:, BANK[f"h{half}"], S * f:S * (f + 1)], ACT.Relu,
                                         bias=b1[:, n:n + 1]).then_inc(h_ready, 1)

            def tanh_z(b, kb):
                act.wait_ge(zh_ready, b + 1)
                if kb > 0:
                    act.wait_ge(g_ready, b)
                nc.scalar.activation(th[:, :], zh[:, :], ACT.Tanh).then_inc(tanh_ready, 1)

            def oT_copy(b, kb, g):
                act.wait_ge(pv_ps, G * b + g + 1)
                if kb > 0 and g == 0:
                    act.wait_ge(o_ps, 2 * b)
                nc.scalar.copy(oT[:, g, :], pv[:, g % 2, 0:S]).then_inc(oT_ready, 1)

            def onT_copy(b, kb):
                act.wait_ge(onT_ps, b + 1)
                if kb > 0:
                    act.wait_ge(s_ps, b)
                nc.scalar.copy(onT[:, :], misc[:, BANK["onT"], 0:S]).then_inc(onT_ready, 1)

            WORK = [
                (0, xnT_copies), (51, onT_copy), (33, hidden, 0), (40, hidden, 1), (6, high), (8, middle),
                (43, tanh_z), *((PASS2 + 3 * g + 6, oT_copy, g) for g in range(G)),
            ]

            def iteration(t, known):
                for step in range(STEPS):
                    for b, kb, (_, u) in at_step(SECOND_PASS, step, t, known):
                        exponentials(b, kb, u)
                    for b, kb, (_, what, *args) in at_step(WORK, step, t, known):
                        what(b, kb, *args)

            iterations(act, iteration)

        @block.gpsimd
        def _(pool):
            pool.wait_ge(consts_loaded, 48)

            def low_x(b, kb):
                pool.wait_ge(xnT_ready, b + 1)
                pool.wait_ge(xnT_hi_ready, b + 1)
                if kb >= AHEAD:
                    pool.wait_ge(h_ps, 2 * (b - AHEAD + 1))
                pool.tensor_tensor(xnT_lo[:, kb % AHEAD, :], xnT[:, kb % 2, :], xnT_hi[:, kb % AHEAD, :],
                                   ALU.subtract).then_inc(xnT_lo_ready, 1)

            def rotate(b, kb, i):
                pool.wait_ge(qk_ready, 2 * b + i + 1)
                pair = lambda t, o: t[:, i, :].rearrange("p (n e h) -> p n e h", e=2, h=H)[:, :, o, :]
                table = lambda a, n: rope[:, i, a:a + n].unsqueeze(2).broadcast_to([P, n, H])
                if kb > 0:
                    pool.wait_ge(rotated, 2 * (b - 1) + i + 1)
                pool.tensor_tensor(rot_a[:, i, :].rearrange("p (n h) -> p n h", h=H),
                                   qk[:, i, :].rearrange("p (n h) -> p n h", h=H), table(0, 2 * DK), ALU.mult
                                   ).then_inc(rope_terms, 1)
                pool.tensor_tensor(pair(rot_b, 0), pair(qk, 1), table(2 * DK, DK), ALU.mult).then_inc(rope_terms, 1)
                pool.tensor_tensor(pair(rot_b, 1), pair(qk, 0), table(3 * DK, DK), ALU.mult).then_inc(rope_terms, 1)
                pool.wait_ge(rope_terms, 6 * b + 3 * i + 3)
                if kb > 0:
                    pool.wait_ge(part_hi, b)
                    pool.wait_ge(part_rem, b)
                pool.tensor_tensor(rot[:, i, :], rot_a[:, i, :], rot_b[:, i, :], ALU.add).then_inc(rotated, 1)

            rot_flat = rot[:, :, :].rearrange("p i n -> p (i n)")
            rem_flat = rem[:, :, :].rearrange("p i n -> p (i n)")

            def parts_flat(c):
                return parts[:, c, :, :, :].rearrange("p i s n -> p (i s n)")

            def remainder(b, kb):
                pool.wait_ge(part_hi, b + 1)
                pool.wait_ge(rotated, 2 * b + 2)
                if kb > 0:
                    pool.wait_ge(part_lo, b)
                    pool.wait_ge(part_mid, b)
                pool.tensor_tensor(rem_flat, rot_flat, parts_flat(0), ALU.subtract).then_inc(part_rem, 1)

            def low(b, kb):
                pool.wait_ge(part_mid, b + 1)
                pool.wait_ge(part_rem, b + 1)
                pool.tensor_tensor(parts_flat(2), rem_flat, parts_flat(1), ALU.subtract).then_inc(part_lo, 1)

            def causal(b, kb, u):
                if UNITS[u][1] != UNITS[u][2]:
                    return
                pool.wait_ge(exp_ready, NU * b + u + 1)
                pool.sem_inc(exp_seen, 1)
                nc.gpsimd.affine_select(out=probs[:, u, :, :], in_=probs[:, u, :, :], pattern=[[0, 4], [1, P]],
                                        compare_op=ALU.is_ge, fill=0.0, base=0, channel_multiplier=-1
                                        ).then_inc(causal_ready, 1)

            WORK = [(1, low_x), (2, rotate, 0), (4, rotate, 1), (7, remainder), (8, low)]

            def iteration(t, known):
                for step in range(STEPS):
                    for b, kb, (_, u) in at_step(SECOND_PASS, step, t, known):
                        causal(b, kb, u)
                    for b, kb, (_, what, *args) in at_step(WORK, step, t, known):
                        what(b, kb, *args)

            iterations(pool, iteration)


def kernel(L0_attn_x, L0_attn_w_qkv, L0_attn_b_qkv, L0_attn_w_out, L0_attn_b_out, L0_ffn_W1, L0_ffn_b1,
           L0_ffn_W2, L0_ffn_b2):
    import numpy as np
    import concourse.bacc as bacc
    from concourse.bass_utils import run_bass_kernel_spmd

    x = np.ascontiguousarray(L0_attn_x)
    B, S, D = x.shape
    F = L0_ffn_W1.shape[0]
    tall = np.ascontiguousarray
    ident = np.eye(P, dtype=np.float32)
    mask = np.where(np.arange(P)[None, :] > np.arange(P)[:, None], np.float32(MASKED), np.float32(0))
    freq = np.float32(10000.0) ** (-np.arange(0, DK, 2, dtype=np.float32) / np.float32(DK))
    angle = np.arange(S, dtype=np.float32)[:, None] * freq[None, :]
    cos, sin = np.cos(angle), np.sin(angle)
    rope = np.concatenate([np.tile(np.repeat(cos, 2, axis=1), (1, 2)), np.tile(-sin, (1, 2)), np.tile(sin, (1, 2))], axis=1)
    rope = rope.reshape(S // P, P, 4 * DK).transpose(1, 0, 2)
    by_feature = np.arange(D).reshape(D // DK, DK).T.reshape(-1)
    order = np.concatenate([by_feature, D + by_feature, 2 * D + np.arange(D)])
    arrays = {
        "x": x,
        "w_qkv_t": tall(np.asarray(L0_attn_w_qkv)[order].T),
        "b_qkv_all": tall(np.broadcast_to(np.asarray(L0_attn_b_qkv)[order][None, :], (P, 3 * D))),
        "w_out_t": tall(np.asarray(L0_attn_w_out).T),
        "b_out_col": tall(np.asarray(L0_attn_b_out)[:, None]),
        "w1_t": tall(np.asarray(L0_ffn_W1).T),
        "w1_rows": tall(np.asarray(L0_ffn_W1).reshape(F // P, P, D).transpose(1, 0, 2)),
        "b1_cols": tall(np.asarray(L0_ffn_b1).reshape(F // P, P).T),
        "w2_t": tall(np.asarray(L0_ffn_W2).T.reshape(F // P, P, D).transpose(1, 0, 2)),
        "w2_rows": tall(np.asarray(L0_ffn_W2)),
        "b2_col": tall(np.asarray(L0_ffn_b2)[:, None]),
        "ident_in": ident, "mask_in": tall(mask), "rope_in": tall(rope),
    }
    nc = bacc.Bacc("TRN2", target_bir_lowering=False, num_devices=1)
    args = [nc.dram_tensor(n, a.shape, mybir.dt.from_np(a.dtype), kind="ExternalInput").ap() for n, a in arrays.items()]
    args.append(nc.dram_tensor("y", x.shape, F32, kind="ExternalOutput").ap())
    attention_ffn_gate(nc, *args)
    return run_bass_kernel_spmd(nc, [arrays], core_ids=[0]).results[0]["y"]
```

```python
from contextlib import ExitStack

import concourse.bass as bass
from concourse import mybir

F32 = mybir.dt.float32
BF16 = mybir.dt.bfloat16
F16 = mybir.dt.float16
ALU = mybir.AluOpType
ACT = mybir.ActivationFunctionType
AX_X = mybir.AxisListType.X

P = 128
DK = 8
QUAD = 32
LN_EPS = 1e-5
Q_EPS = 1e-5
SUM_EPS = 1e-8
MASKED = -1e30
PARTS = 3
ROWS = DK * PARTS * PARTS
SHIFT_ROWS = ROWS + PARTS
LAGS = 5
AHEAD = 4

STEPS = 12
PASS1 = 20
PASS2 = 37


def attention_ffn_gate(nc, x, w_qkv_t, b_qkv_all, w_out_t, b_out_col, w1_t, w1_rows, b1_cols,
                       w2_t, w2_rows, b2_col, ident_in, mask_in, rope_in, out):
    B, S, D = x.shape
    T = S // P
    H = D // DK
    F = w1_t.shape[1]
    FB = F // P
    G = H // 4
    SCALE = float(DK) ** -0.5
    NT = B * T
    HEADW = QUAD // 2
    CHUNK = 2 * AHEAD
    CHUNK_STEPS = 2 * CHUNK + 1
    LOOP_FROM = LAGS + 2
    LOOP_END = LOOP_FROM + (B - LOOP_FROM) // AHEAD * AHEAD
    assert T == 2 and D == P and G == 4 and FB == 4 and 3 * G == STEPS

    UNITS = [(g, kb, qb) for g in range(G) for kb, qb in ((0, 0), (0, 1), (1, 1))]
    NU = len(UNITS)

    def head(g, j):
        return 8 * (g // 2) + 2 * j + g % 2

    with ExitStack() as ctx:
        def sb(name, shape, dt=F32):
            return ctx.enter_context(nc.sbuf_tensor(name, shape, dt))

        def sem(name):
            return ctx.enter_context(nc.semaphore(name))

        ident = sb("ident", [P, P])
        ident_bf = sb("ident_bf", [P, P], BF16)
        mask = sb("mask", [P, P])
        mask_bf = sb("mask_bf", [P, P], BF16)
        rope = sb("rope", [P, T, 4 * DK])
        ones = sb("ones", [P, P])
        ones_bf = sb("ones_bf", [PARTS, 4 * S], BF16)
        wqkv = sb("wqkv", [P, 3 * D])
        bqkv = sb("bqkv", [P, 3 * D])
        wout = sb("wout", [P, D])
        bout = sb("bout", [P, 1])
        w1 = sb("w1", [P, F])
        w1n = sb("w1n", [P, FB, D])
        w2 = sb("w2", [P, FB, D])
        w2n = sb("w2n", [P, F])
        b1 = sb("b1", [P, FB])
        b2 = sb("b2", [P, 1])
        wabs = sb("wabs", [P, 2])
        gam = sb("gam", [P, 2])
        thr = sb("thr", [P, 2, 2])
        lowq = sb("lowq", [P, 2, F])
        w1q = sb("w1q", [P, F], F16)
        w2q = sb("w2q", [P, FB, D])
        xs = sb("xs", [P, NT, D])
        stats = sb("stats", [P, NT, 6])
        mv = sb("mv", [P, NT, 2])
        std = sb("std", [P, NT])
        rstd = sb("rstd", [P, NT])
        xn = sb("xn", [P, T, D])
        xnT = sb("xnT", [P, 2, S])
        xnT_hi = sb("xnT_hi", [P, AHEAD, S], F16)
        xnT_lo = sb("xnT_lo", [P, AHEAD, S], F16)
        qk = sb("qk", [P, T, 2 * D])
        vaug = sb("vaug", [P, AHEAD, T, H, 3 * HEADW])
        rot_a = sb("rot_a", [P, T, 2 * D])
        rot_b = sb("rot_b", [P, T, 2 * D])
        rot = sb("rot", [P, T, 2 * D])
        rotT = sb("rotT", [P, 2, S])
        rem = sb("rem", [P, 2, S])
        partsT = sb("partsT", [P, 2, PARTS, S], BF16)
        qstack = sb("qstack", [P, AHEAD, H, S], BF16)
        kstack = sb("kstack", [P, AHEAD, H, S], BF16)
        diag = sb("diag", [P, 2, 512])
        mx = sb("mx", [P, 2, 3, H])
        mrem = sb("mrem", [P, T, H])
        mparts = sb("mparts", [P, T, P // H, H], BF16)
        mT = sb("mT", [PARTS * H, S], BF16)
        probs = sb("probs", [P, NU, 4, P])
        oT = sb("oT", [P, G // 2, S])
        lsum = sb("lsum", [P, T * H])
        linv = sb("linv", [P, T * H])
        onorm = sb("onorm", [P, T, D])
        onT = sb("onT", [P, S])
        hT = sb("hT", [P, FB, S])
        zh = sb("zh", [P, S])
        th = sb("th", [P, S])
        gT = sb("gT", [P, AHEAD, S])
        sg = sb("sg", [P, S])
        res = sb("res", [P, 2, T, D])

        s1 = ctx.enter_context(nc.psum_tensor("s1", [P, 3, 512], F32))
        s2 = ctx.enter_context(nc.psum_tensor("s2", [P, 2, 512], F32))
        pv = ctx.enter_context(nc.psum_tensor("pv", [P, 512], F32))
        misc = ctx.enter_context(nc.psum_tensor("misc", [P, 2, 512], F32))

        x_loaded = [sem(f"x_loaded{i}") for i in range(2)]
        consts_loaded = sem("consts_loaded")
        wqkv_loaded = sem("wqkv_loaded")
        weights_loaded = sem("weights_loaded")
        ones_made = sem("ones_made")
        spread_out = sem("spread_out")
        stacks_loaded = [sem(f"stacks_loaded{i}") for i in range(2)]
        shifts_loaded = sem("shifts_loaded")
        stored = [sem(f"stored{i}") for i in range(2)]
        stack_ones = sem("stack_ones")
        consts_ready = sem("consts_ready")
        abs_ready = sem("abs_ready")
        gamma_sum = sem("gamma_sum")
        quant_step = sem("quant_step")
        weights_ready = sem("weights_ready")
        stat_step = sem("stat_step")
        std_ready = sem("std_ready")
        rstd_ready = sem("rstd_ready")
        xn_ready = sem("xn_ready")
        xnT_ps = sem("xnT_ps")
        xnT_ready = sem("xnT_ready")
        xnT_hi_ready = sem("xnT_hi_ready")
        xnT_lo_ready = sem("xnT_lo_ready")
        qkv_ps = sem("qkv_ps")
        qk_ready = sem("qk_ready")
        v_ready = sem("v_ready")
        v_ones = sem("v_ones")
        mmax_ready = sem("mmax_ready")
        rope_terms = sem("rope_terms")
        rope_own = sem("rope_own")
        rotated = sem("rotated")
        rotT_ps = sem("rotT_ps")
        rotT_ready = sem("rotT_ready")
        part_hi = sem("part_hi")
        part_rem = sem("part_rem")
        part_mid = sem("part_mid")
        part_lo = sem("part_lo")
        s1_ps = sem("s1_ps")
        diag_copied = sem("diag_copied")
        diag_seen = sem("diag_seen")
        diag_masked = sem("diag_masked")
        diag_max_ready = sem("diag_max_ready")
        max_ready = sem("max_ready")
        shift_step = sem("shift_step")
        mT_ps = sem("mT_ps")
        mT_ready = sem("mT_ready")
        s2_ps = sem("s2_ps")
        exp_ready = sem("exp_ready")
        exp_seen = sem("exp_seen")
        causal_ready = sem("causal_ready")
        pv_ps = sem("pv_ps")
        oT_ready = sem("oT_ready")
        o_ps = sem("o_ps")
        sum_ready = sem("sum_ready")
        onorm_ready = sem("onorm_ready")
        onT_ps = sem("onT_ps")
        onT_ready = sem("onT_ready")
        h_ps = sem("h_ps")
        h_ready = sem("h_ready")
        z_ps = sem("z_ps")
        zh_ready = sem("zh_ready")
        tanh_ready = sem("tanh_ready")
        g_ready = sem("g_ready")
        s_ps = sem("s_ps")
        sg_ready = sem("sg_ready")
        sgT_ps = sem("sgT_ps")
        res_ready = sem("res_ready")

        JOBS = [
            (24, "h0", 0, [(h_ready, FB, 2)]),
            (1, "xnT", 1, [(xnT_ready, 1, 1), (xnT_hi_ready, 1, 1)]),
            (62, "back", 0, [(res_ready, 1, 1)]),
            (3, "qkv0", 1, [(qk_ready, 2, 1), (v_ready, 2, 1)]),
            (4, "qkv1", 0, [(qk_ready, 2, 2), (v_ready, 2, 2)]),
            (54, "o", 1, [(onorm_ready, 1, 1)]),
            (31, "h1", 0, [(h_ready, FB, 4)]),
            (8, "rotT", 1, [(rotT_ready, 1, 1), (part_hi, 1, 1)]),
            (57, "onT", 0, [(onT_ready, 1, 1)]),
            (33, "shift", 0, [(mT_ready, 1, 1)]),
            (35, "z", 1, [(zh_ready, 1, 1)]),
            (59, "proj", 1, [(sg_ready, 1, 1)]),
        ]
        BANK = {name: bank for _, name, bank, _ in JOBS}

        def at_step(table, step, t, known):
            for row in table:
                lag = row[0] // STEPS
                if row[0] % STEPS == step and 0 <= known - lag < B:
                    yield t - lag, known - lag, row

        def iterations(eng, body):
            for t in range(LOOP_FROM):
                body(t, t)
            with eng.Fori(LOOP_FROM, LOOP_END - AHEAD + 1, AHEAD) as t0:
                for j in range(AHEAD):
                    body(t0 + j, LOOP_FROM + j)
            for t in range(LOOP_END, B + LAGS):
                body(t, t)

        QUANTISE_AT = (0, 5)
        FIRST_PASS = [(PASS1 + u, u) for u in range(NU)]
        SECOND_PASS = [(PASS2 + u, u) for u in range(NU)]

        scratch = nc.dram_tensor("scratch", [2, 2, PARTS, D, S], BF16, kind="Internal").ap()

        block = ctx.enter_context(nc.Block())

        @block.sync
        def _(sp):
            xt = x.rearrange("b (i p) d -> p (b i) d", p=P)
            sp.dma_start(xs[:, 0:CHUNK, :], xt[:, 0:CHUNK, :]).then_inc(x_loaded[0], 16)
            for dst, src in ((ident, ident_in), (mask, mask_in), (rope, rope_in)):
                sp.dma_start(dst[:], src).then_inc(consts_loaded, 16)
            for dst, src in ((wqkv, w_qkv_t), (bqkv, b_qkv_all)):
                sp.dma_start(dst[:], src).then_inc(wqkv_loaded, 16)
            for dst, src in ((w1, w1_t), (w1n, w1_rows), (w2, w2_t), (w2n, w2_rows), (b1, b1_cols), (b2, b2_col),
                             (wout, w_out_t), (bout, b_out_col)):
                sp.dma_start(dst[:], src).then_inc(weights_loaded, 16)
            sp.dma_start(xs[:, CHUNK:NT, :], xt[:, CHUNK:NT, :]).then_inc(x_loaded[1], 16)
            sp.wait_ge(ones_made, 1)
            wide = ones_bf.shape[1]
            sp.dma_start(kstack[ROWS:SHIFT_ROWS, :, :, :].rearrange("p a (x y) s -> p (a x) (y s)", y=wide // S),
                         ones_bf[:, :].unsqueeze(1).broadcast_to([PARTS, AHEAD * H * S // wide, wide])
                         ).then_inc(stack_ones, 16)

            def spread(b, kb):
                sp.wait_ge(part_lo, b + 1)
                sp.dma_start(scratch[kb % 2].rearrange("i c p s -> p (i c) s"),
                             partsT[:, :, :, :].rearrange("p i c s -> p (i c) s")).then_inc(spread_out, 16)

            def stack(b, kb):
                sp.wait_ge(spread_out, 16 * (b + 1))
                queries, keys = [scratch[kb % 2, side].rearrange("c (d h) s -> c d (h s)", d=DK) for side in range(2)]
                sp.dma_start(kstack[0:ROWS, kb % AHEAD, :, :].rearrange("p h s -> p (h s)"),
                             keys.rearrange("c d n -> (c d) n").unsqueeze(0).broadcast_to([PARTS, PARTS * DK, H * S])
                             ).then_inc(stacks_loaded[kb % 2], 16)
                for c in range(PARTS):
                    rows = slice(DK * PARTS * c, DK * PARTS * (c + 1))
                    sp.dma_start(qstack[rows, kb % AHEAD, :, :].rearrange("p h s -> p (h s)"),
                                 queries[c].unsqueeze(0).broadcast_to([PARTS, DK, H * S])
                                 ).then_inc(stacks_loaded[kb % 2], 16)

            def shift(b, kb):
                sp.wait_ge(mT_ready, b + 1)
                sp.dma_start(qstack[ROWS:SHIFT_ROWS, kb % AHEAD, :, :], mT[:, :]).then_inc(shifts_loaded, 16)

            def store(b, kb):
                sp.wait_ge(res_ready, b + 1)
                sp.dma_start(out[bass.ds(b, 1), :, :].rearrange("o (i p) d -> p (o i) d", p=P),
                             res[:, kb % 2, :, :]).then_inc(stored[kb % 2], 16)

            WORK = [(33, shift), (63, store), (12, spread), (12, stack)]

            def iteration(t, known):
                for step in range(STEPS):
                    for b, kb, (_, what, *args) in at_step(WORK, step, t, known):
                        what(b, kb, *args)

            iterations(sp, iteration)
            for s in stored:
                sp.wait_ge(s, 16 * B // 2)

        @block.tensor
        def _(pe):
            def mean_weights():
                pe.wait_ge(abs_ready, 3)
                nc.tensor.matmul(pv[:, 0:2], ones[:, :], wabs[:, :], start=True, stop=True).then_inc(gamma_sum, 1)

            def job_bank(bank, step, t, known):
                for back in range(1, 4 * STEPS):
                    then, it = (step - back) % STEPS, (step - back) // STEPS
                    jobs = [(b, readers) for b, _, (_, _, used, readers) in at_step(JOBS, then, t + it, known + it)
                            if used == bank]
                    for b, readers in jobs:
                        for s, per, at in readers:
                            pe.wait_ge(s, per * b + at)
                    if jobs:
                        return

            def job(name, b, kb):
                bank = misc[:, BANK[name], :]
                buf = kb % AHEAD
                if name == "xnT":
                    if kb == 0:
                        pe.wait_ge(consts_loaded, 48)
                    pe.wait_ge(xn_ready, 2 * b + 2)
                    for i in range(T):
                        mm = nc.tensor.transpose(bank[:, P * i:P * (i + 1)], xn[:, i, :], ident[:, :])
                    mm.then_inc(xnT_ps, 1)
                elif name in ("qkv0", "qkv1"):
                    i = int(name[-1])
                    if kb == 0:
                        pe.wait_ge(wqkv_loaded, 32)
                    pe.wait_ge(xnT_ready, b + 1)
                    nc.tensor.matmul(bank[:, 0:3 * D], xnT[:, kb % 2, P * i:P * (i + 1)], wqkv[:, :],
                                     start=True, stop=True).then_inc(qkv_ps, 1)
                elif name == "rotT":
                    pe.wait_ge(rotated, 2 * b + 2)
                    for side in range(2):
                        for i in range(T):
                            mm = nc.tensor.transpose(bank[:, S * side + P * i:S * side + P * (i + 1)],
                                                     rot[:, i, D * side:D * (side + 1)], ident[:, :])
                    mm.then_inc(rotT_ps, 1)
                elif name == "shift":
                    pe.wait_ge(shift_step, 4 * b + 4)
                    dst = bank.bitcast(BF16)
                    for i in range(T):
                        mm = nc.tensor.transpose(dst[:, 2 * S + P * i:2 * S + P * (i + 1)],
                                                 mparts[:, i, :, :].rearrange("p c h -> p (c h)"), ident_bf[:, :])
                    mm.then_inc(mT_ps, 1)
                elif name in ("h0", "h1"):
                    if kb == 0:
                        pe.wait_ge(weights_ready, 2)
                    pe.wait_ge(xnT_lo_ready, b + 1)
                    pe.wait_ge(xnT_hi_ready, b + 1)
                    for f in range(2):
                        w = w1q[:, P * (2 * int(name[-1]) + f):P * (2 * int(name[-1]) + f + 1)]
                        for k, part in enumerate((xnT_hi, xnT_lo)):
                            mm = nc.tensor.matmul(bank[:, S * f:S * (f + 1)], w, part[:, buf, :],
                                                  start=k == 0, stop=k == 1)
                    mm.then_inc(h_ps, 1)
                elif name == "z":
                    for f in range(FB):
                        if f % 2 == 0:
                            pe.wait_ge(h_ready, FB * b + f + 2)
                        mm = nc.tensor.matmul(bank[:, 0:S], w2q[:, f, :], hT[:, f, :], start=f == 0, stop=f == FB - 1)
                    mm.then_inc(z_ps, 1)
                elif name == "o":
                    pe.wait_ge(oT_ready, G // 2 * (b + 1))
                    for i in range(T):
                        for m in range(G // 2):
                            mm = nc.tensor.transpose(bank[:, S * i + P * m:S * i + P * (m + 1)],
                                                     oT[:, m, P * i:P * (i + 1)], ident[:, :])
                    mm.then_inc(o_ps, 1)
                elif name == "onT":
                    pe.wait_ge(onorm_ready, b + 1)
                    for i in range(T):
                        mm = nc.tensor.transpose(bank[:, P * i:P * (i + 1)], onorm[:, i, :], ident[:, :])
                    mm.then_inc(onT_ps, 1)
                elif name == "proj":
                    if kb == 0:
                        pe.wait_ge(weights_loaded, 128)
                    pe.wait_ge(onT_ready, b + 1)
                    nc.tensor.matmul(bank[:, S:2 * S], wout[:, :], onT[:, :], start=True, stop=True).then_inc(s_ps, 1)
                elif name == "back":
                    pe.wait_ge(sg_ready, b + 1)
                    for i in range(T):
                        mm = nc.tensor.transpose(bank[:, P * i:P * (i + 1)], sg[:, P * i:P * (i + 1)], ident[:, :])
                    mm.then_inc(sgT_ps, 1)

            def pass1(b, kb, u):
                g, key, query = UNITS[u]
                if u == 0 and kb == 0:
                    pe.wait_ge(consts_ready, 2)
                if u == 0:
                    pe.wait_ge(stacks_loaded[kb % 2], 16 * (1 + PARTS) // 2 * (b - kb % 2) + 16 * (1 + PARTS))
                if kb > 0 or u >= 3:
                    if key == query == 0:
                        pe.wait_ge(diag_copied, G * b + g)
                    else:
                        pe.wait_ge(max_ready, 2 * (G * b + g - 1) + u % 3)
                bank = s1[:, u % 3, :]
                masked = key == query == 1
                if masked:
                    nc.tensor.matmul(bank.rearrange("p (h k) -> p h k", h=4), ident_bf[:, :],
                                     mask_bf[:, :].unsqueeze(1).broadcast_to([P, 4, P]), start=True, stop=False)
                for j in range(4):
                    h = head(g, j)
                    mm = nc.tensor.matmul(bank[:, P * j:P * (j + 1)],
                                          qstack[0:ROWS, kb % AHEAD, h, P * query:P * (query + 1)],
                                          kstack[0:ROWS, kb % AHEAD, h, P * key:P * (key + 1)],
                                          start=not masked, stop=not masked or j == 3)
                mm.then_inc(s1_ps, 1)

            def pass2(b, kb, u):
                g, key, query = UNITS[u]
                if u == 0:
                    if kb == 0:
                        pe.wait_ge(stack_ones, 16)
                    pe.wait_ge(shifts_loaded, 16 * (b + 1))
                if kb > 0 or u >= 2:
                    pe.wait_ge(exp_ready, NU * b + u - 1)
                for j in range(4):
                    h = head(g, j)
                    mm = nc.tensor.matmul(s2[:, u % 2, P * j:P * (j + 1)],
                                          kstack[0:SHIFT_ROWS, kb % AHEAD, h, P * key:P * (key + 1)],
                                          qstack[0:SHIFT_ROWS, kb % AHEAD, h, P * query:P * (query + 1)],
                                          start=True, stop=True)
                mm.then_inc(s2_ps, 1)

            def weigh(b, kb, g):
                pe.wait_ge(causal_ready, 2 * G * b + 2 * g + 2)
                pe.wait_ge(exp_ready, NU * b + 3 * g + 3)
                pe.wait_ge(v_ready, 2 * b + 2)
                m, half = g // 2, g % 2
                if half == 0 and (kb > 0 or m > 0):
                    pe.wait_ge(oT_ready, G // 2 * b + m)
                cols = slice(HEADW, 3 * HEADW) if half == 0 else slice(0, 2 * HEADW)
                for j in range(4):
                    nc.tensor.matmul(pv[QUAD * j:QUAD * (j + 1), 0:S], vaug[:, kb % AHEAD, 0, head(g, j), cols],
                                     probs[:, 3 * g:3 * g + 2, j, :], start=half == 0, stop=False)
                for j in range(4):
                    mm = nc.tensor.matmul(pv[QUAD * j:QUAD * (j + 1), P:S], vaug[:, kb % AHEAD, 1, head(g, j), cols],
                                          probs[:, 3 * g + 2, j, :], start=False, stop=half == 1)
                mm.then_inc(pv_ps, 1)

            WEIGH = [(PASS2 + 3 * g + 5, weigh, g) for g in range(G)]

            def iteration(t, known):
                for step in range(STEPS):
                    for b, kb, (_, u) in at_step(FIRST_PASS, step, t, known):
                        pass1(b, kb, u)
                    for b, kb, (_, u) in at_step(SECOND_PASS, step, t, known):
                        pass2(b, kb, u)
                    for b, kb, (_, what, *args) in at_step(WEIGH, step, t, known):
                        what(b, kb, *args)
                    claimed = set()
                    for b, kb, (_, name, bank, _) in at_step(JOBS, step, t, known):
                        if bank not in claimed:
                            job_bank(bank, step, t, known)
                            claimed.add(bank)
                        job(name, b, kb)
                    if (known, step) == QUANTISE_AT:
                        mean_weights()

            iterations(pe, iteration)

        @block.vector
        def _(dve):
            dve.memset(mparts[:, :, :, :], 0.0).then_inc(mmax_ready, 1)
            dve.memset(ones[:, :], 1.0).then_inc(abs_ready, 1)
            dve.memset(ones_bf[:, :], 1.0).then_inc(ones_made, 1)

            def statistics(n):
                tiles = range(CHUNK * n, CHUNK * (n + 1))
                dve.wait_ge(x_loaded[min(n, 1)], 16)
                for tile in tiles:
                    nc.vector.bn_stats(stats[:, tile, :], xs[:, tile, :]).then_inc(stat_step, 1)
                dve.wait_ge(stat_step, CHUNK_STEPS * n + CHUNK)
                for tile in tiles:
                    nc.vector.bn_aggr(mv[:, tile, :], stats[:, tile, :]).then_inc(stat_step, 1)
                dve.wait_ge(stat_step, CHUNK_STEPS * n + 2 * CHUNK)
                chunk = mv[:, CHUNK * n:CHUNK * (n + 1), 1]
                dve.tensor_scalar(chunk, chunk, LN_EPS, None, ALU.add).then_inc(stat_step, 1)

            def inverse_std(n):
                chunk = slice(CHUNK * n, CHUNK * (n + 1))
                dve.wait_ge(std_ready, n + 1)
                nc.vector.reciprocal(rstd[:, chunk], std[:, chunk]).then_inc(rstd_ready, 1)
                dve.wait_ge(rstd_ready, n + 1)

            def quantise():
                dve.wait_ge(weights_loaded, 128)
                nc.vector.tensor_reduce(wabs[:, 0:1], w1n[:, :, :], axis=mybir.AxisListType.XY, op=ALU.add,
                                        apply_absolute_value=True).then_inc(abs_ready, 1)
                nc.vector.tensor_reduce(wabs[:, 1:2], w2n[:, :], axis=AX_X, op=ALU.add,
                                        apply_absolute_value=True).then_inc(abs_ready, 1)
                dve.wait_ge(gamma_sum, 1)
                dve.tensor_scalar(gam[:, :], pv[:, 0:2], 1.0 / (F * D), Q_EPS, ALU.mult, ALU.add).then_inc(quant_step, 1)
                dve.wait_ge(quant_step, 1)
                dve.tensor_scalar(thr[:, 0, :], gam[:, :], 0.5, None, ALU.mult).then_inc(quant_step, 1)
                dve.tensor_scalar(thr[:, 1, :], gam[:, :], -0.5, None, ALU.mult).then_inc(quant_step, 1)
                dve.wait_ge(quant_step, 3)
                w2flat = w2[:, :, :].rearrange("p f d -> p (f d)")
                w2qflat = w2q[:, :, :].rearrange("p f d -> p (f d)")
                for n, (w, q) in enumerate(((w1[:, :], w1q[:, :]), (w2flat, w2qflat))):
                    dve.tensor_scalar(lowq[:, n, :], w, thr[:, 1, n:n + 1], None, ALU.is_lt).then_inc(quant_step, 1)
                    dve.wait_ge(quant_step, 4 + n)
                    nc.vector.scalar_tensor_tensor(q, w, thr[:, 0, n:n + 1], lowq[:, n, :], ALU.is_gt,
                                                   ALU.subtract).then_inc(weights_ready, 1)

            def low_precision_constants():
                dve.wait_ge(consts_loaded, 48)
                dve.tensor_copy(ident_bf[:, :], ident[:, :]).then_inc(consts_ready, 1)
                dve.tensor_copy(mask_bf[:, :], mask[:, :]).then_inc(consts_ready, 1)

            PROLOGUE = [
                ((0, 5), low_precision_constants), (QUANTISE_AT, quantise), ((0, 5), statistics, 1),
                ((1, 1), inverse_std, 1), ((1, 1), statistics, 2), ((1, 6), inverse_std, 2), ((1, 6), statistics, 3),
                ((2, 1), inverse_std, 3),
            ]

            statistics(0)
            inverse_std(0)

            def maxima(b, kb, u):
                g, key, query = UNITS[u]
                if key == query == 0:
                    return
                dve.wait_ge(s1_ps, NU * b + u + 1)
                maxima_of(b, kb, g, u % 3, s1[:, u % 3, :]).then_inc(max_ready, 1)

            def diagonal_maxima(b, kb, g):
                dve.wait_ge(diag_masked, G * b + g + 1)
                if g == 0 and kb > 1:
                    dve.wait_ge(shift_step, 4 * (b - 1))
                maxima_of(b, kb, g, 0, diag[:, g % 2, :]).then_inc(diag_max_ready, 1)

            def maxima_of(b, kb, g, kind, scores):
                slot = (0, 2, 1)[kind]
                return nc.vector.tensor_reduce(mx[:, kb % 2, slot, head(g, 0):head(g, 3) + 1:2],
                                               scores.rearrange("p (h k) -> p h k", h=4), axis=AX_X, op=ALU.max)

            def normalise(b, kb):
                if kb > 0:
                    dve.wait_ge(xnT_ps, b)
                for i in range(T):
                    tile = T * b + i
                    ti = bass.ds(tile, 1)
                    dve.tensor_scalar(xn[:, i:i + 1, :], xs[:, ti, :], mv_of(tile), rstd_of(tile),
                                      ALU.subtract, ALU.mult).then_inc(xn_ready, 1)

            def mv_of(tile):
                return mv[:, bass.ds(tile, 1), 0]

            def rstd_of(tile):
                return rstd[:, bass.ds(tile, 1)]

            def qkv(b, kb, i):
                if kb == 0 and i == 0:
                    dve.wait_ge(wqkv_loaded, 32)
                dve.wait_ge(qkv_ps, 2 * b + i + 1)
                if kb > 0:
                    dve.wait_ge(rotated, 2 * (b - 1) + i + 1)
                bank = misc[:, BANK[f"qkv{i}"], :]
                dve.tensor_tensor(qk[:, i, :], bank[:, 0:2 * D], bqkv[:, 0:2 * D], ALU.add).then_inc(qk_ready, 1)
                if kb == 0 and i == 0:
                    dve.wait_ge(v_ones, 2)
                if kb >= AHEAD:
                    dve.wait_ge(pv_ps, G * (b - AHEAD + 1))
                dve.tensor_tensor(vaug[:, kb % AHEAD, i, :, HEADW:HEADW + DK],
                                  bank[:, 2 * D:3 * D].rearrange("p (h d) -> p h d", d=DK),
                                  bqkv[:, 2 * D:3 * D].rearrange("p (h d) -> p h d", d=DK), ALU.add).then_inc(v_ready, 1)
                dve.wait_ge(qk_ready, 2 * b + i + 1)
                dve.tensor_tensor(rot_a[:, i, :].rearrange("p (n h) -> p n h", h=H),
                                  qk[:, i, :].rearrange("p (n h) -> p n h", h=H),
                                  rope[:, i, 0:2 * DK].unsqueeze(2).broadcast_to([P, 2 * DK, H]), ALU.mult
                                  ).then_inc(rope_own, 1)

            def shift(b, kb):
                dve.wait_ge(max_ready, 2 * G * (b + 1))
                dve.wait_ge(diag_max_ready, G * (b + 1))
                if kb > 0:
                    dve.wait_ge(mT_ps, b)
                dve.tensor_tensor(mx[:, kb % 2, 1, :], mx[:, kb % 2, 1, :], mx[:, kb % 2, 2, :], ALU.max).then_inc(mmax_ready, 1)
                dve.wait_ge(mmax_ready, b + 2)
                m = mx[:, kb % 2, 0:2, :]
                dve.tensor_scalar(mparts[:, :, 0, :], m, -1.0, None, ALU.mult).then_inc(shift_step, 1)
                dve.wait_ge(shift_step, 4 * b + 1)
                nc.vector.scalar_tensor_tensor(mrem[:, :, :], m, -1.0, mparts[:, :, 0, :], ALU.mult,
                                               ALU.subtract).then_inc(shift_step, 1)
                dve.wait_ge(shift_step, 4 * b + 2)
                dve.tensor_copy(mparts[:, :, 1, :], mrem[:, :, :]).then_inc(shift_step, 1)
                dve.wait_ge(shift_step, 4 * b + 3)
                dve.tensor_tensor(mparts[:, :, 2, :], mrem[:, :, :], mparts[:, :, 1, :], ALU.subtract).then_inc(shift_step, 1)

            def onorm_make(b, kb):
                dve.wait_ge(o_ps, b + 1)
                heads = misc[:, BANK["o"], :].rearrange("p (n w) -> p n w", w=HEADW)
                if kb > 0:
                    dve.wait_ge(onT_ps, b)
                dve.tensor_scalar(lsum[:, :], heads[:, :, DK], SUM_EPS, None, ALU.add).then_inc(sum_ready, 1)
                dve.wait_ge(sum_ready, 2 * b + 1)
                nc.vector.reciprocal(linv[:, :], lsum[:, :]).then_inc(sum_ready, 1)
                dve.wait_ge(sum_ready, 2 * b + 2)
                dve.tensor_tensor(onorm[:, :, :].rearrange("p i (h d) -> p (i h) d", d=DK), heads[:, :, 0:DK],
                                  linv[:, :].unsqueeze(2).broadcast_to([P, T * H, DK]), ALU.mult).then_inc(onorm_ready, 1)

            def half_z(b, kb):
                dve.wait_ge(z_ps, b + 1)
                dve.tensor_scalar(zh[:, :], misc[:, BANK["z"], 0:S], b2[:, :], 0.5, ALU.add, ALU.mult).then_inc(zh_ready, 1)

            def silu(b, kb):
                dve.wait_ge(zh_ready, b + 1)
                dve.wait_ge(tanh_ready, b + 1)
                nc.vector.scalar_tensor_tensor(gT[:, kb % AHEAD, :], th[:, :], 1.0, zh[:, :],
                                               ALU.add, ALU.mult).then_inc(g_ready, 1)

            def gate(b, kb):
                dve.wait_ge(s_ps, b + 1)
                if kb > 0:
                    dve.wait_ge(sgT_ps, b)
                nc.vector.scalar_tensor_tensor(sg[:, :], misc[:, BANK["proj"], S:2 * S], bout[:, :], gT[:, kb % AHEAD, :],
                                               ALU.add, ALU.mult).then_inc(sg_ready, 1)

            def residual(b, kb):
                dve.wait_ge(sgT_ps, b + 1)
                if kb >= 2:
                    dve.wait_ge(stored[kb % 2], 8 * (b - kb % 2))
                dve.tensor_tensor(res[:, kb % 2, :, :], xs[:, bass.ds(T * b, T), :],
                                  misc[:, BANK["back"], 0:S].rearrange("p (i d) -> p i d", i=T), ALU.add).then_inc(res_ready, 1)

            WORK = [
                (0, normalise), (62, residual), (3, qkv, 0), (4, qkv, 1),
                *((PASS1 + 3 * g + 2, diagonal_maxima, g) for g in range(G)),
                (54, onorm_make), (31, shift), (59, gate), (35, half_z), (37, silu),
            ]

            def iteration(t, known):
                for step in range(STEPS):
                    for b, kb, (_, u) in at_step(FIRST_PASS, step, t, known):
                        maxima(b, kb, u)
                    for b, kb, (_, what, *args) in at_step(WORK, step, t, known):
                        what(b, kb, *args)
                    for at, what, *args in PROLOGUE:
                        if (known, step) == at:
                            what(*args)

            iterations(dve, iteration)

        @block.scalar
        def _(act):
            def deviation(n):
                chunk = slice(CHUNK * n, CHUNK * (n + 1))
                act.wait_ge(stat_step, CHUNK_STEPS * (n + 1))
                nc.scalar.activation(std[:, chunk], mv[:, chunk, 1], ACT.Sqrt).then_inc(std_ready, 1)

            deviation(0)

            def exponentials(b, kb, u):
                g = u // 3
                act.wait_ge(s2_ps, NU * b + u + 1)
                if kb > 0:
                    act.wait_ge(pv_ps, G * (b - 1) + g + 1)
                nc.scalar.activation(probs[:, u, :, :].rearrange("p h q -> p (h q)"), s2[:, u % 2, :], ACT.Exp,
                                     scale=SCALE).then_inc(exp_ready, 1)

            def diagonal_copy(b, kb, g):
                act.wait_ge(s1_ps, NU * b + 3 * g + 1)
                if kb > 0 or g >= 2:
                    act.wait_ge(diag_max_ready, G * b + g - 1)
                nc.scalar.copy(diag[:, g % 2, :], s1[:, 0, :]).then_inc(diag_copied, 1)

            def xnT_copies(b, kb):
                src = misc[:, BANK["xnT"], 0:S]
                act.wait_ge(xnT_ps, b + 1)
                if kb >= 2:
                    act.wait_ge(qkv_ps, 2 * (b - 1))
                    act.wait_ge(xnT_lo_ready, b - 1)
                nc.scalar.copy(xnT[:, kb % 2, :], src).then_inc(xnT_ready, 1)
                if kb >= AHEAD:
                    act.wait_ge(h_ps, 2 * (b - AHEAD + 1))
                nc.scalar.copy(xnT_hi[:, kb % AHEAD, :], src).then_inc(xnT_hi_ready, 1)

            def rotT_copy(b, kb):
                act.wait_ge(rotT_ps, b + 1)
                if kb > 0:
                    act.wait_ge(part_rem, b)
                nc.scalar.copy(rotT[:, :, :], misc[:, BANK["rotT"], :].rearrange("p (i s) -> p i s", i=2)
                               ).then_inc(rotT_ready, 1)

            def high(b, kb):
                if kb > 0:
                    act.wait_ge(spread_out, 16 * b)
                nc.scalar.copy(partsT[:, :, 0, :], misc[:, BANK["rotT"], :].rearrange("p (i s) -> p i s", i=2)
                               ).then_inc(part_hi, 1)

            def middle(b, kb):
                act.wait_ge(part_rem, b + 1)
                nc.scalar.copy(partsT[:, :, 1, :], rem[:, :, :]).then_inc(part_mid, 1)

            def hidden(b, kb, half):
                act.wait_ge(h_ps, 2 * b + half + 1)
                if kb > 0 and half == 0:
                    act.wait_ge(z_ps, b)
                for f in range(2):
                    n = 2 * half + f
                    nc.scalar.activation(hT[:, n, :], misc[:, BANK[f"h{half}"], S * f:S * (f + 1)], ACT.Relu,
                                         bias=b1[:, n:n + 1]).then_inc(h_ready, 1)

            def tanh_z(b, kb):
                act.wait_ge(zh_ready, b + 1)
                if kb > 0:
                    act.wait_ge(g_ready, b)
                nc.scalar.activation(th[:, :], zh[:, :], ACT.Tanh).then_inc(tanh_ready, 1)

            def oT_copy(b, kb, m):
                act.wait_ge(pv_ps, G * b + 2 * m + 2)
                if kb > 0 and m == 0:
                    act.wait_ge(o_ps, b)
                nc.scalar.copy(oT[:, m, :], pv[:, 0:S]).then_inc(oT_ready, 1)

            def mT_copy(b, kb):
                act.wait_ge(mT_ps, b + 1)
                if kb > 0:
                    act.wait_ge(shifts_loaded, 16 * b)
                nc.scalar.copy(mT[:, :], misc[0:PARTS * H, BANK["shift"], :].bitcast(BF16)[:, 2 * S:3 * S]).then_inc(mT_ready, 1)

            def onT_copy(b, kb):
                act.wait_ge(onT_ps, b + 1)
                if kb > 0:
                    act.wait_ge(s_ps, b)
                nc.scalar.copy(onT[:, :], misc[:, BANK["onT"], 0:S]).then_inc(onT_ready, 1)

            WORK = [
                *((PASS1 + 3 * g, diagonal_copy, g) for g in range(G)), (1, xnT_copies), (8, rotT_copy), (8, high), (33, mT_copy), (57, onT_copy), (10, middle), (24, hidden, 0), (31, hidden, 1),
                (36, tanh_z), *((PASS2 + 6 * m + 9, oT_copy, m) for m in range(G // 2)),
            ]

            def iteration(t, known):
                for step in range(STEPS):
                    for b, kb, (_, u) in at_step(SECOND_PASS, step, t, known):
                        exponentials(b, kb, u)
                    for b, kb, (_, what, *args) in at_step(WORK, step, t, known):
                        what(b, kb, *args)
                    for n, at in enumerate(((0, 10), (1, 5), (1, 10)), 1):
                        if (known, step) == at:
                            deviation(n)

            iterations(act, iteration)

        @block.gpsimd
        def _(pool):
            pool.memset(vaug[:, :, :, :, :], 0.0).then_inc(v_ones, 1)
            pool.wait_ge(v_ones, 1)
            pool.memset(vaug[:, :, :, :, HEADW + DK:HEADW + DK + 1], 1.0).then_inc(v_ones, 1)
            pool.wait_ge(consts_loaded, 48)

            def low_x(b, kb):
                pool.wait_ge(xnT_ready, b + 1)
                pool.wait_ge(xnT_hi_ready, b + 1)
                if kb >= AHEAD:
                    pool.wait_ge(h_ps, 2 * (b - AHEAD + 1))
                pool.tensor_tensor(xnT_lo[:, kb % AHEAD, :], xnT[:, kb % 2, :], xnT_hi[:, kb % AHEAD, :],
                                   ALU.subtract).then_inc(xnT_lo_ready, 1)

            def rotate(b, kb, i):
                pool.wait_ge(qk_ready, 2 * b + i + 1)
                pair = lambda t, o: t[:, i, :].rearrange("p (n e h) -> p n e h", e=2, h=H)[:, :, o, :]
                table = lambda a, n: rope[:, i, a:a + n].unsqueeze(2).broadcast_to([P, n, H])
                if kb > 0:
                    pool.wait_ge(rotated, 2 * (b - 1) + i + 1)
                pool.tensor_tensor(pair(rot_b, 0), pair(qk, 1), table(2 * DK, DK), ALU.mult).then_inc(rope_terms, 1)
                pool.tensor_tensor(pair(rot_b, 1), pair(qk, 0), table(3 * DK, DK), ALU.mult).then_inc(rope_terms, 1)
                pool.wait_ge(rope_terms, 4 * b + 2 * i + 2)
                pool.wait_ge(rope_own, 2 * b + i + 1)
                if kb > 0:
                    pool.wait_ge(rotT_ps, b)
                pool.tensor_tensor(rot[:, i, :], rot_a[:, i, :], rot_b[:, i, :], ALU.add).then_inc(rotated, 1)

            def remainder(b, kb):
                pool.wait_ge(part_hi, b + 1)
                pool.wait_ge(rotT_ready, b + 1)
                if kb > 0:
                    pool.wait_ge(part_lo, b)
                    pool.wait_ge(part_mid, b)
                pool.tensor_tensor(rem[:, :, :], rotT[:, :, :], partsT[:, :, 0, :], ALU.subtract).then_inc(part_rem, 1)

            def low(b, kb):
                pool.wait_ge(part_mid, b + 1)
                pool.wait_ge(part_rem, b + 1)
                pool.tensor_tensor(partsT[:, :, 2, :], rem[:, :, :], partsT[:, :, 1, :], ALU.subtract).then_inc(part_lo, 1)

            def causal(b, kb, u):
                if UNITS[u][1] != UNITS[u][2]:
                    return
                pool.wait_ge(exp_ready, NU * b + u + 1)
                pool.sem_inc(exp_seen, 1)
                nc.gpsimd.affine_select(out=probs[:, u, :, :], in_=probs[:, u, :, :], pattern=[[0, 4], [1, P]],
                                        compare_op=ALU.is_ge, fill=0.0, base=0, channel_multiplier=-1
                                        ).then_inc(causal_ready, 1)

            def mask_scores(b, kb, g):
                pool.wait_ge(diag_copied, G * b + g + 1)
                pool.sem_inc(diag_seen, 1)
                nc.gpsimd.affine_select(out=diag[:, g % 2, :].rearrange("p (h k) -> p h k", h=4),
                                        in_=diag[:, g % 2, :].rearrange("p (h k) -> p h k", h=4), pattern=[[0, 4], [-1, P]],
                                        compare_op=ALU.is_ge, fill=MASKED, base=0, channel_multiplier=1
                                        ).then_inc(diag_masked, 1)

            WORK = [
                (11, low), *((PASS1 + 3 * g, mask_scores, g) for g in range(G)), (22, low_x), (3, rotate, 0),
                (4, rotate, 1), (9, remainder),
            ]

            def iteration(t, known):
                for step in range(STEPS):
                    for b, kb, (_, u) in at_step(SECOND_PASS, step, t, known):
                        causal(b, kb, u)
                    for b, kb, (_, what, *args) in at_step(WORK, step, t, known):
                        what(b, kb, *args)

            iterations(pool, iteration)


def kernel(L0_attn_x, L0_attn_w_qkv, L0_attn_b_qkv, L0_attn_w_out, L0_attn_b_out, L0_ffn_W1, L0_ffn_b1,
           L0_ffn_W2, L0_ffn_b2):
    import numpy as np
    import concourse.bacc as bacc
    from concourse.bass_utils import run_bass_kernel_spmd

    x = np.ascontiguousarray(L0_attn_x)
    B, S, D = x.shape
    F = L0_ffn_W1.shape[0]
    tall = np.ascontiguousarray
    ident = np.eye(P, dtype=np.float32)
    mask = np.where(np.arange(P)[None, :] > np.arange(P)[:, None], np.float32(MASKED), np.float32(0))
    freq = np.float32(10000.0) ** (-np.arange(0, DK, 2, dtype=np.float32) / np.float32(DK))
    angle = np.arange(S, dtype=np.float32)[:, None] * freq[None, :]
    cos, sin = np.cos(angle), np.sin(angle)
    rope = np.concatenate([np.tile(np.repeat(cos, 2, axis=1), (1, 2)), np.tile(-sin, (1, 2)), np.tile(sin, (1, 2))], axis=1)
    rope = rope.reshape(S // P, P, 4 * DK).transpose(1, 0, 2)
    by_feature = np.arange(D).reshape(D // DK, DK).T.reshape(-1)
    order = np.concatenate([by_feature, D + by_feature, 2 * D + np.arange(D)])
    arrays = {
        "x": x,
        "w_qkv_t": tall(np.asarray(L0_attn_w_qkv)[order].T),
        "b_qkv_all": tall(np.broadcast_to(np.asarray(L0_attn_b_qkv)[order][None, :], (P, 3 * D))),
        "w_out_t": tall(np.asarray(L0_attn_w_out).T),
        "b_out_col": tall(np.asarray(L0_attn_b_out)[:, None]),
        "w1_t": tall(np.asarray(L0_ffn_W1).T),
        "w1_rows": tall(np.asarray(L0_ffn_W1).reshape(F // P, P, D).transpose(1, 0, 2)),
        "b1_cols": tall(np.asarray(L0_ffn_b1).reshape(F // P, P).T),
        "w2_t": tall(np.asarray(L0_ffn_W2).T.reshape(F // P, P, D).transpose(1, 0, 2)),
        "w2_rows": tall(np.asarray(L0_ffn_W2)),
        "b2_col": tall(np.asarray(L0_ffn_b2)[:, None]),
        "ident_in": ident, "mask_in": tall(mask), "rope_in": tall(rope),
    }
    nc = bacc.Bacc("TRN2", target_bir_lowering=False, num_devices=1)
    args = [nc.dram_tensor(n, a.shape, mybir.dt.from_np(a.dtype), kind="ExternalInput").ap() for n, a in arrays.items()]
    args.append(nc.dram_tensor("y", x.shape, F32, kind="ExternalOutput").ap())
    attention_ffn_gate(nc, *args)
    return run_bass_kernel_spmd(nc, [arrays], core_ids=[0]).results[0]["y"]
```
